# Optimizing a Trainium2 kernel written in Bass

```python
import numpy as np
import jax
import jax.numpy as jnp

def _softmax(x, axis=-1):
    return jax.nn.softmax(x, axis=axis)
def _gelu(x):
    return jax.nn.gelu(x, approximate=True)
def _silu(x):
    return jax.nn.silu(x)
def _sigmoid(x):
    return jax.nn.sigmoid(x)
def _layernorm(x, axis=-1, eps=1e-5):
    m = jnp.mean(x, axis=axis, keepdims=True)
    v = jnp.var(x, axis=axis, keepdims=True)
    return (x - m) / jnp.sqrt(v + eps)
def _scatter_add(tgt, idx, src, axis=0):
    return tgt.at[idx].add(src)
def _segment_sum(src, seg, n):
    return jax.ops.segment_sum(src, seg, n)

kernel_name = 'mk_conv_seq_d1_conv_nchw512_ab39b2'

def setup_inputs(seed: int = 0):
    np.random.seed(seed)
    _w = jnp.asarray
    def _rec_inputs():
        import jax
        import jax.numpy as jnp
        _gk = jax.random.key(seed)
        x = 7.22e-05 + 1 * jax.random.normal(jax.random.fold_in(_gk, 1), (16, 512, 32, 32), jnp.float32)
        return x
    x = _rec_inputs()
    def _L0_conv_setup():
        import jax, jax.numpy as jnp
        import numpy as np
        HEADS = 8
        HEAD_DIM = 64
        SCALE = HEAD_DIM ** (-0.5)
        key = jax.random.key(seed)
        k1, k2, k3, k4 = jax.random.split(key, 4)
        B, C, H, W = (16, 512, 32, 32)
        hidden = HEADS * HEAD_DIM
        return {'x': jax.random.normal(k1, (B, C, H, W), dtype=jnp.float32), 'w_qkv': jax.random.normal(k2, (3 * hidden, C), dtype=jnp.float32) * 0.02, 'w_out': jax.random.normal(k3, (C, hidden), dtype=jnp.float32) * 0.02, 'b_out': jax.random.normal(k4, (C,), dtype=jnp.float32) * 0.02, 'rms_scale': jnp.ones((C,), dtype=jnp.float32)}
    _L0_conv_all = _L0_conv_setup()
    _L0_conv_in = {k: v for k, v in _L0_conv_all.items() if k in ('w_qkv', 'w_out', 'b_out', 'rms_scale', )}
    del _L0_conv_all

    return {
        "x": x,
        "L0_conv_w_qkv": _L0_conv_in["w_qkv"],
        "L0_conv_w_out": _L0_conv_in["w_out"],
        "L0_conv_b_out": _L0_conv_in["b_out"],
        "L0_conv_rms_scale": _L0_conv_in["rms_scale"],
    }

def reference(x, L0_conv_w_qkv, L0_conv_w_out, L0_conv_b_out, L0_conv_rms_scale):
    import jax
    import jax.numpy as jnp
    def _L0_conv_ref(x, w_qkv, w_out, b_out, rms_scale):
        import jax, jax.numpy as jnp
        import numpy as np
        HEADS = 8
        HEAD_DIM = 64
        SCALE = HEAD_DIM ** (-0.5)
        b, c, H, W = x.shape
        n = H * W
        qkv = jnp.einsum('bchw,oc->bohw', x, w_qkv)
        q, k, v = jnp.split(qkv, 3, axis=1)
        q = q.reshape(b, HEADS, HEAD_DIM, n) * SCALE
        k = k.reshape(b, HEADS, HEAD_DIM, n)
        v = v.reshape(b, HEADS, HEAD_DIM, n)
        sim = jnp.einsum('bhdi,bhdj->bhij', q, k)
        attn = jax.nn.softmax(sim, axis=-1)
        out = jnp.einsum('bhij,bhdj->bhid', attn, v)
        out = out.transpose(0, 1, 3, 2).reshape(b, HEADS * HEAD_DIM, H, W)
        y = jnp.einsum('bchw,oc->bohw', out, w_out) + b_out[None, :, None, None]
        mean_sq = jnp.mean(y * y, axis=1, keepdims=True)
        y = y * jax.lax.rsqrt(mean_sq + SCALE) * rms_scale[None, :, None, None]
        return y + x

    def _gn(v, G=32, eps=1e-5):
        B_, C_, H_, W_ = v.shape
        g = v.reshape(B_, G, C_ // G, H_, W_)
        m = jnp.mean(g, axis=(2, 3, 4), keepdims=True)
        s = jnp.var(g, axis=(2, 3, 4), keepdims=True)
        return ((g - m) / jnp.sqrt(s + eps)).reshape(v.shape)

    def _ln_c(v, eps=1e-6):
        m = jnp.mean(v, axis=1, keepdims=True)
        s = jnp.var(v, axis=1, keepdims=True)
        return (v - m) / jnp.sqrt(s + eps)

    def _ln_t(v, eps=1e-5):
        m = jnp.mean(v, axis=-1, keepdims=True)
        s = jnp.var(v, axis=-1, keepdims=True)
        return (v - m) / jnp.sqrt(s + eps)

    def _to_tokens(v):
        B_, C_, H_, W_ = v.shape
        return v.reshape(B_, C_, H_ * W_).transpose(0, 2, 1)
    def _from_tokens(t, like):
        B_, C_, H_, W_ = like.shape
        return t.transpose(0, 2, 1).reshape(B_, C_, H_, W_)

    x = _L0_conv_ref(x, L0_conv_w_qkv, L0_conv_w_out, L0_conv_b_out, L0_conv_rms_scale)
    return x


_drawn_inputs = setup_inputs


def setup_inputs(seed=0):
    import zlib

    import numpy as np

    out = dict(_drawn_inputs(seed))
    spreads = {'L0_conv_rms_scale': (1.0, 0.6)}
    factors = {'L0_conv_w_qkv': 2.878, 'L0_conv_w_out': 2.851}
    for name, (base, spread) in spreads.items():
        noise = np.random.default_rng([zlib.crc32(name.encode()), seed]).standard_normal(out[name].shape)
        drawn = base * np.exp(spread * noise) if base else spread * noise
        out[name] = jnp.asarray(drawn.astype(out[name].dtype))
    for name, factor in factors.items():
        out[name] = (out[name] * factor).astype(out[name].dtype)
    return out
```

```python
from contextlib import ExitStack

import numpy as np

import concourse.bass as bass
from concourse import mybir

F32 = mybir.dt.float32
F32R = mybir.dt.float32r
ACT = mybir.ActivationFunctionType
ALU = mybir.AluOpType
AX_X = mybir.AxisListType.X

P = 128

SLOTS, STEPS = 8, 8


def items_at(slot, j, first, last):
    pair, half = divmod(slot, 2)
    following = not (last and slot == SLOTS - 1)
    preceding = not (first and slot == 0)
    out = []
    if j == 0 and following:
        out += ["Q"] + (["K"] if slot == 7 else [])
    if j == 1:
        out += ["L"] if preceding else []
        out += ["K"] if half == 0 and pair < 3 else []
        out += {1: ["V0"], 3: ["V1"], 7: ["V0"] if following else []}.get(slot, [])
    if following:
        out += {2: ["M0"], 3: ["M1", "M2"], 4: ["M3", "M4"], 5: ["M5", "M6"], 6: ["M7"]}.get(j, [])
    if j == 2 and slot in (1, 2) and not first:
        out.append("R")
    if j == 3 and slot == 7 and following:
        out.append("V1")
    if preceding:
        out += {6: ["O0"]}.get(j, [])
    if j == 7:
        out += (["T"] if following else []) + (["O1"] if preceding else [])
    return out


PRO_ITEMS = ["Q", "K", "V0", "V1"] + [f"M{i}" for i in range(8)] + ["T"]
EPI_ITEMS = ["L", "O0", "O1", "R0", "R1"]


class AuxCounts:

    def __init__(self, names, start):
        self.start, self.place = list(start), {}
        used, at = list(start), (start[0] + start[1]) % 2
        for key in names:
            self.place[key] = (at, used[at] - start[at])
            used[at] += 1
            at ^= 1
        self.end = used


def body_keys(first, last):
    return [(s, n) for s in range(SLOTS) for j in range(STEPS) for n in items_at(s, j, first, last)]


def attention_kernel(nc, x, wqkv, wout, bias, scale, consts, out):
    B, C, N = x.shape
    HID = wout.shape[0] * wout.shape[1]
    D = 64
    HEADS = HID // D
    PAIRS = HEADS // 2
    KT = C // P
    MT = C // P
    JT = N // P
    HALF = N // 2
    IT = HALF // P
    WCOLS = 2 * P
    SOFT = float(D) ** -0.5
    assert PAIRS * 2 == SLOTS and JT == STEPS and N == 1024 and C == 512

    VA, VB = 4, 5
    RING_OF = {0: 0, VB: 0, VA: 1, 2: 1, 1: 2, 3: 2}

    pro = AuxCounts([(7, n) for n in PRO_ITEMS], (0, 0))
    body0 = AuxCounts(body_keys(True, False), pro.end)
    loop = AuxCounts(body_keys(False, False), body0.end)
    per_batch = (loop.end[0] - loop.start[0], loop.end[1] - loop.start[1])
    assert per_batch[0] == per_batch[1]
    LOOPS = B - 2
    bodyz = AuxCounts(body_keys(False, True), [s + LOOPS * n for s, n in zip(loop.start, per_batch)])
    epi = AuxCounts([(0, n) for n in EPI_ITEMS], bodyz.end)

    ctx = ExitStack()
    with ctx:
        def sb(name, shape, dt=F32):
            return ctx.enter_context(nc.sbuf_tensor(name, shape, dt))

        def psum(name, shape):
            return ctx.enter_context(nc.psum_tensor(name, shape, F32))

        def sem(name):
            return ctx.enter_context(nc.semaphore(name))

        x_stage = sb("x_stage", [P, 2, HALF])
        x_hi = sb("x_hi", [P, KT, N], F32R)
        x_lo = sb("x_lo", [P, KT, N], F32R)
        w_ring = sb("w_ring", [P, 3, 2, KT, WCOLS], F32R)
        wo_hi = sb("wo_hi", [P, PAIRS, C], F32R)
        wo_lo = sb("wo_lo", [P, PAIRS, C], F32R)
        q_hl = sb("q_hl", [P, 2, 2, HALF], F32R)
        q_hm = sb("q_hm", [P, 2, 2, HALF], F32R)
        k_hh = sb("k_hh", [P, 2, 2, N], F32R)
        k_l1 = sb("k_l1", [P, 2, 2, N], F32R)
        v_sb = sb("v_sb", [P, 2, JT, WCOLS])
        probs = sb("probs", [P, STEPS // 2, 2, HALF])
        prob_sum = sb("prob_sum", [P, 2, HALF])
        o_norm = sb("o_norm", [P, HALF])
        o_hi = sb("o_hi", [P, HALF], F32R)
        o_lo = sb("o_lo", [P, HALF], F32R)
        y_sb = sb("y_sb", [P, 2, MT, HALF])
        inv_sum = sb("inv_sum", [P, HALF])
        sq_a = sb("sq_a", [P, HALF])
        sq_b = sb("sq_b", [P, HALF])
        rms_a = sb("rms_a", [P, HALF])
        rms_b = sb("rms_b", [P, HALF])
        resid = sb("resid", [P, MT, HALF])
        neg_ident = sb("neg_ident", [P, P])
        tile_mask = sb("tile_mask", [IT, HALF])
        ones_d = sb("ones_d", [P, D])
        ones_c = sb("ones_c", [P, P])
        bias_sb = sb("bias_sb", [P, MT])
        scale_sb = sb("scale_sb", [P, MT])
        maxima = sb("maxima", [P, 2 * IT])

        y_flat = y_sb[:].rearrange("p h m n -> p (h m n)")
        p_flat = probs[:].rearrange("p a e n -> p (a e n)")
        W1 = KT * WCOLS
        raw_at = {0: y_flat[:, 0:W1], VA: y_flat[:, W1:2 * W1], 1: p_flat[:, 2 * W1:3 * W1],
                  2: p_flat[:, 3 * W1:4 * W1], 3: y_flat[:, 0:W1], VB: y_flat[:, W1:2 * W1]}
        raw_wo = p_flat[:, 0:2 * W1]
        spill = y_flat[:, 2 * W1:4 * W1].bitcast(F32R)

        w_split = nc.dram_tensor("w_split", [6, P, 2 * W1], F32, kind="Internal").ap()

        score = [psum(f"score{e}", [P, HALF]) for e in range(2)]
        pv = [psum(f"pv{h}", [P, HALF]) for h in range(2)]
        aux = [psum(f"aux{i}", [P, 2 * HALF]) for i in range(2)]

        aux_full = [sem("aux_full0"), sem("aux_full1")]
        aux_free = [sem("aux_free0"), sem("aux_free1")]
        score_ready = sem("score_ready")
        prob_ready = sem("prob_ready")
        pv_done = sem("pv_done")
        prob_added = sem("prob_added")
        hi_ready = sem("hi_ready")
        onorm_ready = sem("onorm_ready")
        ohi_ready = sem("ohi_ready")
        olo_ready = sem("olo_ready")
        sq_step = sem("sq_step")
        ms_ready = sem("ms_ready")
        inv_ms_ready = sem("inv_ms_ready")
        rinv_ready = sem("rinv_ready")
        y_scaled = sem("y_scaled")
        resid_added = sem("resid_added")
        resid_loaded = [sem(f"resid_loaded{i}") for i in range(MT)]
        out_stored = sem("out_stored")
        x_loaded = [sem("x_loaded0"), sem("x_loaded1")]
        xhi_ready = sem("xhi_ready")
        x_split = sem("x_split")
        w_loaded = [sem(f"w_loaded{i}") for i in range(3)]
        raw_loaded = {c: sem(f"raw_loaded{c}") for c in range(6)}
        raw_wo_loaded = sem("raw_wo_loaded")
        const_loaded = sem("const_loaded")
        const_set = sem("const_set")
        w_hi_set = sem("w_hi_set")
        w_set = sem("w_set")
        spill_hi_set = sem("spill_hi_set")
        spill_set = sem("spill_set")
        wo_set = sem("wo_set")
        spilled = sem("spilled")
        spilled_t = sem("spilled_t")

        x_v = x.rearrange("b (k p) n -> b k p n", p=P)
        out_v = out.rearrange("b (k p) n -> b k p n", p=P)

        def aux_counts(plan, b, key):
            at, n = plan.place[key]
            if plan is loop:
                return at, (b - 1) * per_batch[at] + plan.start[at] + n
            return at, plan.start[at] + n

        class Body:

            def __init__(self, plan, b, first, last):
                self.plan, self.b, self.first, self.last = plan, b, first, last

            def at(self, slot, name):
                return aux_counts(self.plan, self.b, (slot, name))

            def full(self, eng, slot, name):
                at, n = self.at(slot, name)
                eng.wait_ge(aux_full[at], n + 1)
                return at

            def consumed(self, eng, slot, name):
                at, n = self.at(slot, name)
                eng.wait_ge(aux_free[at], n + 1)

        def run_bodies(eng, one):
            one(Body(body0, 0, True, False))
            with eng.Fori(1, 1 + LOOPS) as b:
                one(Body(loop, b, False, False))
            one(Body(bodyz, B - 1, False, True))

        def earlier_at(body, slot, name):
            if body.plan is body0:
                plan, start = pro, pro.start
            elif body.plan is epi:
                plan, start = bodyz, bodyz.start
            else:
                at, n = loop.place[(slot, name)]
                base = body.plan.start[at] + ((body.b - 1) * per_batch[at] if body.plan is loop else 0)
                return at, base - (per_batch[at] - n)
            at, n = plan.place[(slot, name)]
            return at, start[at] + n

        def wait_items(eng, what, places):
            for at, n in dict(places).items():
                eng.wait_ge(what[at], n + 1)

        block = ctx.enter_context(nc.Block())

        @block.sync
        def _(sp):
            sp.dma_start(raw_at[0], wqkv[0]).then_inc(raw_loaded[0], 16)
            for c in range(2):
                sp.dma_start(x_stage[:, c, :], x_v[0, c // 2, :, (c % 2) * HALF:(c % 2 + 1) * HALF]
                             ).then_inc(x_loaded[c], 16)
            sp.dma_start(neg_ident[:], consts[:, 0:P]).then_inc(const_loaded, 16)
            sp.dma_start(tile_mask[:], consts[0:IT, P:P + HALF]).then_inc(const_loaded, 16)
            sp.dma_start(bias_sb[:], bias).then_inc(const_loaded, 16)
            sp.dma_start(scale_sb[:], scale).then_inc(const_loaded, 16)
            for c in range(2, 2 * KT):
                sp.wait_ge(x_split, c - 1)
                sp.dma_start(x_stage[:, c % 2, :],
                             x_v[0, c // 2, :, (c % 2) * HALF:(c % 2 + 1) * HALF]
                             ).then_inc(x_loaded[c % 2], 16)
                if c == 2:
                    sp.dma_start(raw_at[VA], wqkv[VA]).then_inc(raw_loaded[VA], 16)
                if c == 4:
                    sp.dma_start(raw_at[1], wqkv[1]).then_inc(raw_loaded[1], 16)
                    sp.dma_start(raw_wo, wout.rearrange("p a n -> p (a n)")
                                 ).then_inc(raw_wo_loaded, 16)
                    sp.dma_start(raw_at[2], wqkv[2]).then_inc(raw_loaded[2], 16)
            for n, c in enumerate((0, VA, 1)):
                sp.wait_ge(w_set, n + 1)
                sp.dma_start(w_split[c], w_ring[:, RING_OF[c]].rearrange("p h k n -> p (h k n)").bitcast(F32)
                             ).then_inc(spilled, 16)
                if c != 1:
                    late = {0: 3, VA: VB}[c]
                    sp.dma_start(raw_at[late], wqkv[late]).then_inc(raw_loaded[late], 16)
            for n, c in enumerate((2, 3, VB)):
                sp.wait_ge(spill_set, n + 1)
                sp.dma_start(w_split[c], spill.bitcast(F32)).then_inc(spilled_t, 16)
            sp.wait_ge(spilled, 48)
            sp.wait_ge(spilled_t, 48)

            def load_w(c):
                ring = RING_OF[c]
                sp.dma_start(w_ring[:, ring].rearrange("p h k n -> p (h k n)").bitcast(F32), w_split[c]
                             ).then_inc(w_loaded[ring], 16)

            def load_x(b, c):
                sp.dma_start(x_stage[:, c % 2, :],
                             x_v[b, c // 2, :, (c % 2) * HALF:(c % 2 + 1) * HALF]
                             ).then_inc(x_loaded[c % 2], 16)

            def finish_half(b, half, body_after=None):
                done = b * 2 + half
                cols = slice(half * HALF, (half + 1) * HALF)
                if half == 1 or body_after is None:
                    sp.wait_ge(out_stored, 16 * MT * done)
                for m in range(MT):
                    sp.dma_start(resid[:, m, :], x_v[b, m, :, cols]).then_inc(resid_loaded[m], 16)
                for m in range(MT):
                    sp.wait_ge(resid_added, 4 * done + m + 1)
                    sp.dma_start(out_v[b, m, :, cols], resid[:, m, :]).then_inc(out_stored, 16)

            def one(body):
                b = body.b
                wait_items(sp, aux_full, [earlier_at(body, 7, "V1")])
                load_w(2)
                body.full(sp, 0, "Q")
                load_w(VB)
                if not body.first:
                    finish_half(b - 1, 0, body)
                body.full(sp, 2, "Q")
                load_w(3)
                if not body.first:
                    finish_half(b - 1, 1, body)
                if not body.last:
                    body.full(sp, 3, "V1")
                    load_w(0)
                    body.full(sp, 4, "Q")
                    load_w(VA)
                    sp.wait_ge(x_split, 2 * KT * (b + 1))
                    load_x(b + 1, 0)
                    if not body.first:
                        sp.wait_ge(out_stored, 16 * MT * 2 * b)
                    load_x(b + 1, 1)
                    body.full(sp, 6, "Q")
                    load_w(1)
                    for c in range(2, 2 * KT):
                        sp.wait_ge(x_split, 2 * KT * (b + 1) + c - 1)
                        load_x(b + 1, c)

            run_bodies(sp, one)
            finish_half(B - 1, 0)
            finish_half(B - 1, 1)
            sp.wait_ge(out_stored, 16 * MT * 2 * B)

        @block.tensor
        def _(pe):
            def claim(body, slot, name, after=()):
                at, n = body.at(slot, name)
                if not (body.plan is pro and n == 0):
                    pe.wait_ge(aux_free[at], n)
                wait_items(pe, aux_free, [(a, i) for a, i in (body.at(*key) for key in after) if a != at])
                return at

            def wait_w(body, chunk, next_batch):
                ring = RING_OF[chunk]
                if body.plan is pro:
                    pe.wait_ge(w_set, {0: 1, VA: 2}[chunk])
                elif chunk in (0, 1, VA):
                    if body.first and not next_batch:
                        pe.wait_ge(w_set, 3)
                    else:
                        pe.wait_ge(w_loaded[ring], 16 * (2 * (body.b + (1 if next_batch else 0))))
                else:
                    pe.wait_ge(w_loaded[ring], 16 * (2 * body.b + 1))

            def project(out_ap, w, cols, xcols):
                n = 0
                for k in range(KT):
                    for wp, xp in ((0, x_hi), (1, x_hi), (0, x_lo)):
                        last = pe.matmul(out_ap, w[:, wp, k, cols], xp[:, k, xcols],
                                         start=(n == 0), stop=(n == 3 * KT - 1))
                        n += 1
                return last

            def item(body, slot, name):
                nslot = (slot + 1) % SLOTS
                npair, nhalf = divmod(nslot, 2)
                nb = slot == 7
                if name == "Q":
                    at = claim(body, slot, name)
                    if slot == 7:
                        pe.wait_ge(x_split, 2 * KT * (body.b + 2))
                    wait_w(body, npair, nb)
                    project(aux[at][:, 0:HALF], w_ring[:, RING_OF[npair]], slice(0, P),
                            slice(nhalf * HALF, (nhalf + 1) * HALF)).then_inc(aux_full[at], 1)
                elif name == "K":
                    kpair = (slot // 2 + 1) % PAIRS
                    at = claim(body, slot, name)
                    wait_w(body, kpair, nb)
                    for h in range(2):
                        last = project(aux[at][:, h * HALF:(h + 1) * HALF],
                                       w_ring[:, RING_OF[kpair]], slice(P, 2 * P),
                                       slice(h * HALF, (h + 1) * HALF))
                    last.then_inc(aux_full[at], 1)
                elif name in ("V0", "V1"):
                    chunk = VA if nb else VB
                    at = claim(body, slot, name)
                    wait_w(body, chunk, nb)
                    w = w_ring[:, RING_OF[chunk]]
                    for i in range(JT // 2):
                        jt = int(name[1]) * (JT // 2) + i
                        n = 0
                        for k in range(KT):
                            for wp, xp in ((0, x_hi), (1, x_hi), (0, x_lo)):
                                last = pe.matmul(aux[at][:, i * WCOLS:(i + 1) * WCOLS],
                                                 xp[:, k, jt * P:(jt + 1) * P], w[:, wp, k, :],
                                                 start=(n == 0), stop=(n == 3 * KT - 1))
                                n += 1
                    last.then_inc(aux_full[at], 1)
                elif name[0] == "M":
                    e, it = divmod(int(name[1]), IT)
                    after = []
                    if name == "M0":
                        after = [(slot, "Q")]
                        if nslot == 0:
                            after = [(slot, "Q"), (slot, "K")]
                        elif nhalf == 0:
                            after = [(slot - 1, "K"), (slot, "Q")]
                    at = claim(body, slot, name, after)
                    for h in range(2):
                        last = pe.matmul(aux[at][:, h * HALF:(h + 1) * HALF],
                                         q_hl[:, nhalf, e, it * P:(it + 1) * P],
                                         k_hh[:, npair % 2, e, h * HALF:(h + 1) * HALF],
                                         start=True, stop=True)
                    last.then_inc(aux_full[at], 1)
                elif name == "T":
                    at = claim(body, slot, name, [(slot, "M6"), (slot, "M7")])
                    for e in range(2):
                        last = pe.matmul(aux[at][0:IT, e * P:(e + 1) * P],
                                         maxima[:, e * IT:(e + 1) * IT], neg_ident[:],
                                         start=True, stop=True)
                    last.then_inc(aux_full[at], 1)
                elif name == "L":
                    done = body.b * SLOTS + slot
                    at = claim(body, slot, name)
                    pe.wait_ge(prob_added, 14 * done)
                    for e in range(2):
                        last = pe.matmul(aux[at][e * D:(e + 1) * D, 0:HALF], ones_d[:],
                                         prob_sum[:, e, :], start=True, stop=True)
                    last.then_inc(aux_full[at], 1)
                elif name in ("O0", "O1"):
                    done = body.b * SLOTS + slot
                    pair = (slot - 1) % SLOTS // 2
                    at = claim(body, slot, name)
                    if name == "O0":
                        pe.wait_ge(olo_ready, done)
                        if body.first and slot == 1:
                            pe.wait_ge(wo_set, 1)
                    for i in range(2):
                        m = 2 * int(name[1]) + i
                        for n, (w, o) in enumerate(((wo_hi, o_hi), (wo_lo, o_hi), (wo_hi, o_lo))):
                            last = pe.matmul(aux[at][:, i * HALF:(i + 1) * HALF],
                                             w[:, pair, m * P:(m + 1) * P], o[:],
                                             start=(n == 0), stop=(n == 2))
                    last.then_inc(aux_full[at], 1)
                else:
                    half = int(name[1]) if name != "R" else slot - 1
                    batch = body.b if name in ("R0", "R1") else body.b - 1
                    at = claim(body, slot, name)
                    pe.wait_ge(sq_step, 7 * (2 * batch + half + 1))
                    pe.matmul(aux[at][:, 0:HALF], ones_c[:], sq_a[:], start=True, stop=True
                              ).then_inc(aux_full[at], 1)

            def scores(body, slot, j):
                pair, half = divmod(slot, 2)
                for e in range(2):
                    n = body.b * 128 + slot * 16 + 2 * j + e
                    if not (body.first and slot == 0 and j == 0):
                        pe.wait_ge(prob_ready, n - 1)
                    keys = slice(j * P, (j + 1) * P)
                    pe.matmul(score[e][:], k_hh[:, pair % 2, e, keys], q_hl[:, half, e, :],
                              start=True, stop=False)
                    pe.matmul(score[e][:], k_l1[0:D + IT, pair % 2, e, keys],
                              q_hm[0:D + IT, half, e, :], start=False, stop=True
                              ).then_inc(score_ready, 1)

            def values(body, slot, j, back):
                pair, half = divmod(slot, 2)
                b = body.b - 1 if back else body.b
                for e in range(2):
                    n = b * 128 + slot * 16 + 2 * j + e
                    pe.wait_ge(prob_ready, n + 1)
                    if j == 0 and e == 0 and not (body.first and slot < 2):
                        pe.wait_ge(onorm_ready, b * SLOTS + slot - 1)
                    pe.matmul(pv[half][e * D:(e + 1) * D, :],
                              v_sb[:, pair // 2, j, (pair % 2) * P + e * D:(pair % 2) * P + (e + 1) * D],
                              probs[:, j % 4, e, :], start=(j == 0), stop=(j == STEPS - 1)
                              ).then_inc(pv_done, 1)

            def one(body):
                for slot in range(SLOTS):
                    if slot == 0:
                        wait_items(pe, aux_free, [earlier_at(body, 7, n) for n in ("V0", "V1", "T")])
                    elif slot == 4:
                        wait_items(pe, aux_free, [body.at(1, "V0"), body.at(3, "V1"), body.at(3, "T")])
                    else:
                        body.consumed(pe, slot - 1, "T")
                    for j in range(STEPS):
                        scores(body, slot, j)
                        if j > 0:
                            values(body, slot, j - 1, False)
                        elif slot > 0:
                            values(body, slot - 1, STEPS - 1, False)
                        elif not body.first:
                            values(body, SLOTS - 1, STEPS - 1, True)
                        for name in items_at(slot, j, body.first, body.last):
                            item(body, slot, name)

            pe.wait_ge(const_loaded, 64)
            pe.wait_ge(const_set, 3)
            start = Body(pro, -1, True, True)
            for name in PRO_ITEMS:
                item(start, 7, name)
            run_bodies(pe, one)
            end = Body(epi, B, False, True)
            values(end, SLOTS - 1, STEPS - 1, True)
            for name in ("L", "O0", "O1"):
                item(end, 0, name)
            last = Body(epi, B - 1, False, True)
            item(last, 0, "R0")
            item(last, 0, "R1")

        @block.scalar
        def _(act):
            def exponentials(body, slot, j):
                for e in range(2):
                    n = body.b * 128 + slot * 16 + 2 * j + e
                    act.wait_ge(score_ready, n + 1)
                    if not (body.first and slot == 0 and j < 4):
                        act.wait_ge(pv_done, n - 7)
                        base = (body.b * SLOTS + slot) * 14
                        added = base + (2 * max(j - 5, 0) + e + 1 if j >= 4 else 2 * (j + 3) + e + 1 - 14)
                        act.wait_ge(prob_added, added)
                    act.activation(probs[:, j % 4, e, :], score[e][:], ACT.Exp, scale=SOFT
                                   ).then_inc(prob_ready, 1)

            def item(body, slot, name):
                nslot = (slot + 1) % SLOTS
                npair, nhalf = divmod(nslot, 2)
                if name == "Q":
                    at = body.full(act, slot, name)
                    for e in range(2):
                        src = aux[at][e * D:(e + 1) * D, 0:HALF]
                        for dst in (q_hl[0:D, nhalf, e, :], q_hm[0:D, nhalf, e, :]):
                            act.activation(dst, src, ACT.Copy).then_inc(hi_ready, 1)
                elif name == "K":
                    kpair = (slot // 2 + 1) % PAIRS
                    at = body.full(act, slot, name)
                    for e in range(2):
                        src = aux[at][e * D:(e + 1) * D, :]
                        for row in (0, D):
                            act.activation(k_hh[row:row + D, kpair % 2, e, :], src, ACT.Copy
                                           ).then_inc(hi_ready, 1)
                elif name in ("V0", "V1"):
                    at = body.full(act, slot, name)
                    j0 = int(name[1]) * (JT // 2)
                    act.activation(v_sb[:, 0 if slot == 7 else 1, j0:j0 + JT // 2, :],
                                   aux[at][:].rearrange("p (j n) -> p j n", n=WCOLS), ACT.Copy
                                   ).then_inc(aux_free[at], 1)
                elif name in ("O0", "O1") and slot in (1, 2):
                    at = body.full(act, slot, name)
                    half = slot - 1
                    if name == "O0" and not body.first:
                        act.wait_ge(resid_added, 4 * (2 * (body.b - 1) + half + 1))
                    if name == "O0" and body.first and half == 0:
                        act.wait_ge(spilled_t, 48)
                    for i in range(2):
                        m = 2 * int(name[1]) + i
                        ins = act.activation(y_sb[:, half, m, :], aux[at][:, i * HALF:(i + 1) * HALF],
                                             ACT.Identity, bias=bias_sb[:, m:m + 1])
                    ins.then_inc(aux_free[at], 1)

            def root(done):
                act.wait_ge(inv_ms_ready, done + 1)
                act.activation(rms_a[:], rms_b[:], ACT.Sqrt).then_inc(rinv_ready, 1)

            def split_x(c, n):
                act.wait_ge(x_loaded[c % 2], 16 * (n * KT + c // 2 + 1))
                act.activation(x_hi[:, c // 2, (c % 2) * HALF:(c % 2 + 1) * HALF],
                               x_stage[:, c % 2, :], ACT.Copy).then_inc(xhi_ready, 1)

            def one(body):
                for slot in range(SLOTS):
                    for j in range(STEPS):
                        exponentials(body, slot, j)
                        for name in items_at(slot, j, body.first, body.last):
                            item(body, slot, name)
                        if j == 3 and slot in (1, 2) and not body.first:
                            root(2 * (body.b - 1) + slot - 1)
                        if slot == 6 and not body.last:
                            if j == 0:
                                body.full(act, 6, "Q")
                            split_x(j, body.b + 1)

            for c in range(2 * KT):
                split_x(c, 0)
            start = Body(pro, -1, True, True)
            act.wait_ge(const_loaded, 64)
            for name in PRO_ITEMS:
                item(start, 7, name)
            act.wait_ge(w_set, 3)
            act.wait_ge(wo_set, 1)
            act.wait_ge(spill_set, 1)
            run_bodies(act, one)
            root(2 * (B - 1))
            root(2 * (B - 1) + 1)

        @block.vector
        def _(dve):
            def item(body, slot, name):
                nslot = (slot + 1) % SLOTS
                npair, nhalf = divmod(nslot, 2)
                if name in ("Q", "K"):
                    at = body.full(dve, slot, name)
                    order = [(s, n) for s in range(SLOTS) for j in range(STEPS)
                             for n in items_at(s, j, False, False) if n in "QK"]
                    if body.plan is pro:
                        before = ("Q", "K").index(name)
                    else:
                        before = 12 * body.b + 2 + order.index((slot, name))
                    for e in range(2):
                        rows = slice(e * D, (e + 1) * D)
                        dve.wait_ge(hi_ready, 4 * before + 2 * e + 2)
                        if name == "Q":
                            ins = dve.tensor_tensor(q_hl[D:2 * D, nhalf, e, :], aux[at][rows, 0:HALF],
                                                    q_hl[0:D, nhalf, e, :].bitcast(F32), ALU.subtract)
                        else:
                            kp = (slot // 2 + 1) % PAIRS % 2
                            ins = dve.tensor_tensor(k_l1[0:D, kp, e, :], aux[at][rows, :],
                                                    k_hh[rows, kp, e, :].bitcast(F32), ALU.subtract)
                    ins.then_inc(aux_free[at], 1)
                elif name[0] == "M":
                    at = body.full(dve, slot, name)
                    n = int(name[1])
                    dve.tensor_reduce(maxima[:, n:n + 1], aux[at][:], AX_X, ALU.max
                                      ).then_inc(aux_free[at], 1)
                elif name == "T":
                    at = body.full(dve, slot, name)
                    for e in range(2):
                        ins = dve.tensor_tensor(
                            q_hm[D:D + IT, nhalf, e, :].rearrange("t (i n) -> t i n", i=IT),
                            aux[at][0:IT, e * P:(e + 1) * P].unsqueeze(1).to_broadcast([IT, IT, P]),
                            tile_mask[:].rearrange("t (i n) -> t i n", i=IT), ALU.mult)
                    ins.then_inc(aux_free[at], 1)
                elif name == "L":
                    done = body.b * SLOTS + slot
                    half = (slot - 1) % 2
                    at = body.full(dve, slot, name)
                    dve.reciprocal(inv_sum[:], aux[at][:, 0:HALF]).then_inc(aux_free[at], 1)
                    body.consumed(dve, slot, name)
                    dve.wait_ge(pv_done, 16 * done)
                    dve.tensor_tensor(o_norm[:], inv_sum[:], pv[half][:], ALU.mult
                                      ).then_inc(onorm_ready, 1)
                    dve.wait_ge(onorm_ready, done)
                    dve.tensor_copy(o_hi[:], o_norm[:]).then_inc(ohi_ready, 1)
                    dve.wait_ge(ohi_ready, done)
                    dve.tensor_tensor(o_lo[:], o_norm[:], o_hi[:].bitcast(F32), ALU.subtract
                                      ).then_inc(olo_ready, 1)
                elif name in ("O0", "O1") and slot not in (1, 2):
                    half, m = (slot - 1) % 2, 2 * int(name[1])
                    at = body.full(dve, slot, name)
                    if slot in (3, 4):
                        body.consumed(dve, slot - 2, name)
                    elif slot == 0:
                        wait_items(dve, aux_free, [earlier_at(body, 6, name)])
                    else:
                        body.consumed(dve, slot - 2, name)
                    y = y_sb[:, half, m:m + 2, :].rearrange("p m n -> p (m n)")
                    dve.tensor_tensor(y, y, aux[at][:], ALU.add).then_inc(aux_free[at], 1)
                elif name[0] == "R":
                    half = int(name[1]) if name != "R" else slot - 1
                    batch = body.b if name in ("R0", "R1") else body.b - 1
                    done = 2 * batch + half
                    at = body.full(dve, slot, name)
                    if name == "R1":
                        dve.wait_ge(y_scaled, 4 * done)
                    dve.tensor_scalar(rms_a[:], aux[at][:, 0:HALF], SOFT, None, ALU.add
                                      ).then_inc(aux_free[at], 1)
                    body.consumed(dve, slot, name)
                    dve.reciprocal(rms_b[:], rms_a[:]).then_inc(inv_ms_ready, 1)

            def scale_y(done, half):
                dve.wait_ge(rinv_ready, done + 1)
                for m in range(MT):
                    dve.scalar_tensor_tensor(out=y_sb[:, half, m, :], in0=y_sb[:, half, m, :],
                                             scalar=scale_sb[:, m:m + 1], in1=rms_a[:],
                                             op0=ALU.mult, op1=ALU.mult).then_inc(y_scaled, 1)

            def split_x(c, n):
                dve.wait_ge(xhi_ready, 8 * n + c + 1)
                cols = slice((c % 2) * HALF, (c % 2 + 1) * HALF)
                dve.tensor_tensor(x_lo[:, c // 2, cols], x_stage[:, c % 2, :],
                                  x_hi[:, c // 2, cols].bitcast(F32), ALU.subtract
                                  ).then_inc(x_split, 1)

            def split_w(n, c):
                dve.wait_ge(raw_loaded[c], 16)
                ring = w_ring[:, RING_OF[c]].rearrange("p h k n -> p h (k n)")
                dve.tensor_copy(ring[:, 0], raw_at[c]).then_inc(w_hi_set, 1)
                dve.wait_ge(w_hi_set, n + 1)
                dve.tensor_tensor(ring[:, 1], raw_at[c], ring[:, 0].bitcast(F32), ALU.subtract
                                  ).then_inc(w_set, 1)

            def one(body):
                for slot in range(SLOTS):
                    for j in range(STEPS):
                        for name in items_at(slot, j, body.first, body.last):
                            item(body, slot, name)
                        if j == 4 and slot in (1, 2) and not body.first:
                            scale_y(2 * (body.b - 1) + slot - 1, slot - 1)
                        if slot == 6 and not body.last:
                            split_x(j, body.b + 1)

            dve.memset(ones_d[:], 1.0).then_inc(const_set, 1)
            dve.memset(ones_c[:], 1.0 / C).then_inc(const_set, 1)
            dve.memset(k_l1[D:D + IT].rearrange("p a e n -> p (a e n)").bitcast(F32), 1.0
                       ).then_inc(const_set, 1)
            split_w(0, 0)
            for c in range(2 * KT):
                split_x(c, 0)
                if c == 3:
                    split_w(1, VA)
            split_w(2, 1)
            dve.wait_ge(const_loaded, 64)
            start = Body(pro, -1, True, True)
            for name in PRO_ITEMS:
                item(start, 7, name)
            run_bodies(dve, one)
            end = Body(epi, B, False, True)
            for name in ("L", "O0", "O1"):
                item(end, 0, name)
            last = Body(epi, B - 1, False, True)
            for half in range(2):
                item(last, 0, f"R{half}")
                scale_y(2 * (B - 1) + half, half)

        @block.gpsimd
        def _(pool):
            def add_probs(body, slot, j):
                base = (body.b * SLOTS + slot) * 14
                for e in range(2):
                    n = body.b * 128 + slot * 16 + 2 * j + e
                    pool.wait_ge(prob_ready, n + 1)
                    if j == 1:
                        if e == 0 and not (body.first and slot == 0):
                            body.full(pool, slot, "L")
                        pool.tensor_tensor(prob_sum[:, e, :], probs[:, 0, e, :], probs[:, 1, e, :],
                                           ALU.add).then_inc(prob_added, 1)
                    else:
                        pool.wait_ge(prob_added, base + 2 * (j - 2) + e + 1)
                        pool.tensor_tensor(prob_sum[:, e, :], prob_sum[:, e, :], probs[:, j % 4, e, :],
                                           ALU.add).then_inc(prob_added, 1)

            def square(done, half, k, y_complete):
                if k == 0:
                    y_complete()
                else:
                    pool.wait_ge(sq_step, 7 * done + k)
                if k in (0, 1, 3, 5):
                    m = (k + 1) // 2
                    dst = sq_a if k == 0 else sq_b
                    pool.tensor_tensor(dst[:], y_sb[:, half, m, :], y_sb[:, half, m, :], ALU.mult
                                       ).then_inc(sq_step, 1)
                else:
                    pool.tensor_tensor(sq_a[:], sq_a[:], sq_b[:], ALU.add).then_inc(sq_step, 1)

            def add_resid(done):
                for m in range(MT):
                    pool.wait_ge(y_scaled, 4 * done + m + 1)
                    pool.wait_ge(resid_loaded[m], 16 * (done + 1))
                    pool.tensor_tensor(resid[:, m, :], resid[:, m, :], y_sb[:, done_half[0], m, :],
                                       ALU.add).then_inc(resid_added, 1)

            done_half = [0]

            def one(body):
                for slot in range(SLOTS):
                    for j in range(STEPS):
                        if j:
                            add_probs(body, slot, j)
                        if body.first:
                            continue
                        if slot == 0 and j:
                            def complete():
                                wait_items(pool, aux_free, [earlier_at(body, 7, n) for n in ("O0", "O1")])
                            square(2 * (body.b - 1), 0, j - 1, complete)
                        if slot == 1 and j in (3, 4, 6, 7):
                            def complete():
                                body.full(pool, 1, "R")
                                wait_items(pool, aux_free, [body.at(0, n) for n in ("O0", "O1")])
                            for k in {3: (0, 1), 4: (2, 3), 6: (4, 5), 7: (6,)}[j]:
                                square(2 * (body.b - 1) + 1, 1, k, complete)
                        if j == 5 and slot in (1, 2):
                            done_half[0] = slot - 1
                            add_resid(2 * (body.b - 1) + slot - 1)

            pool.wait_ge(raw_wo_loaded, 16)
            pool.tensor_copy(wo_hi[:].rearrange("p a n -> p (a n)"), raw_wo).then_inc(spill_hi_set, 1)
            pool.wait_ge(spill_hi_set, 1)
            pool.tensor_tensor(wo_lo[:].rearrange("p a n -> p (a n)"), raw_wo,
                               wo_hi[:].rearrange("p a n -> p (a n)").bitcast(F32), ALU.subtract
                               ).then_inc(wo_set, 1)
            for n, c in enumerate((2, 3, VB)):
                pool.wait_ge(raw_loaded[c], 16)
                if n:
                    pool.wait_ge(spilled_t, 16 * n)
                pool.tensor_copy(spill[:, 0:W1], raw_at[c]).then_inc(spill_hi_set, 1)
                pool.wait_ge(spill_hi_set, n + 2)
                pool.tensor_tensor(spill[:, W1:2 * W1], raw_at[c], spill[:, 0:W1].bitcast(F32),
                                   ALU.subtract).then_inc(spill_set, 1)
            run_bodies(pool, one)
            end = Body(epi, B, False, True)
            last = Body(epi, B - 1, False, True)
            for k in range(7):
                square(2 * (B - 1), 0, k, lambda: wait_items(
                    pool, aux_free, [earlier_at(end, 7, n) for n in ("O0", "O1")]))

            def complete():
                last.full(pool, 0, "R0")
                wait_items(pool, aux_free, [end.at(0, n) for n in ("O0", "O1")])
            for k in range(7):
                square(2 * (B - 1) + 1, 1, k, complete)
            for half in range(2):
                done_half[0] = half
                add_resid(2 * (B - 1) + half)


def kernel(x, L0_conv_w_qkv, L0_conv_w_out, L0_conv_b_out, L0_conv_rms_scale):
    import concourse.bacc as bacc
    from concourse.bass_utils import run_bass_kernel_spmd

    x = np.ascontiguousarray(x)
    b, c, h, w = x.shape
    w_qkv, w_out = np.asarray(L0_conv_w_qkv), np.asarray(L0_conv_w_out)
    hid = w_out.shape[1]
    pairs = hid // P

    def chunk(rows):
        a = w_qkv[rows].reshape(len(rows), c // P, P)
        return a.transpose(2, 1, 0).reshape(P, -1)

    chunks = [chunk(np.r_[p * P:(p + 1) * P, hid + p * P:hid + (p + 1) * P]) for p in range(pairs)]
    chunks += [chunk(np.r_[2 * hid + s * 2 * P:2 * hid + (s + 1) * 2 * P]) for s in range(2)]
    consts = np.zeros((P, P + h * w // 2), np.float32)
    consts[:, 0:P] = -np.eye(P, dtype=np.float32)
    for t in range(h * w // 2 // P):
        consts[t, P + t * P:P + (t + 1) * P] = 1.0
    arrays = {
        "x": x.reshape(b, c, h * w),
        "wqkv": np.ascontiguousarray(np.stack(chunks)),
        "wout": np.ascontiguousarray(w_out.T.reshape(pairs, P, c).transpose(1, 0, 2)),
        "bias": np.ascontiguousarray(np.asarray(L0_conv_b_out).reshape(c // P, P).T),
        "scale": np.ascontiguousarray(np.asarray(L0_conv_rms_scale).reshape(c // P, P).T),
        "consts": consts,
    }
    nc = bacc.Bacc("TRN2", target_bir_lowering=False, num_devices=1)
    args = [nc.dram_tensor(n, a.shape, mybir.dt.from_np(a.dtype), kind="ExternalInput").ap()
            for n, a in arrays.items()]
    out = nc.dram_tensor("out", (b, c, h * w), F32, kind="ExternalOutput").ap()
    attention_kernel(nc, *args, out)
    r = run_bass_kernel_spmd(nc, [arrays], core_ids=[0])
    return r.results[0]["out"].reshape(b, c, h, w)
```

```python
from contextlib import ExitStack

import numpy as np

import concourse.bass as bass
from concourse import mybir

F32 = mybir.dt.float32
F32R = mybir.dt.float32r
ACT = mybir.ActivationFunctionType
ALU = mybir.AluOpType
AX_X = mybir.AxisListType.X

P = 128

SLOTS, STEPS = 8, 8
HALF_STEPS = 2 * STEPS
SQUARE_AT = (3, 5, 8, 10)
SPLIT_AT = (1, 2, 3, 5, 8, 9, 10, 11)


def items_at(slot, t, first, last):
    following = not (last and slot == SLOTS - 1)
    preceding = not (first and slot == 0)
    out = []
    if t == 0 and following:
        out.append("Q")
    if t == 1 and preceding:
        out.append("L")
    if following:
        maxima = (4, 5, 6, 7, 8, 9, 10, 11)
        out += [f"M{maxima.index(t)}"] if t in maxima else []
        if slot == 7:
            out += {2: ["K"], 3: ["V0"], 15: ["V1"]}.get(t, [])
    if t == 3:
        out += {1: ["V0"], 2: ["V1"]}.get(slot, [])
    if t == 12 and preceding:
        out.append("O0")
    if t == 13 and following:
        out.append("T")
    if t == 14 and preceding:
        out.append("O1")
    if t == 15 and slot in (0, 1) and not first:
        out.append("R")
    if t == 15 and slot in (0, 2, 4):
        out.append("K")
    return out


PRO_ITEMS = ["Q", "K", "V0", "V1"] + [f"M{i}" for i in range(8)] + ["T"]
EPI_ITEMS = ["L", "O0", "O1", "R0", "R1"]


class AuxCounts:

    def __init__(self, names, start):
        self.start, self.place = list(start), {}
        used, at = list(start), (start[0] + start[1]) % 2
        for key in names:
            self.place[key] = (at, used[at] - start[at])
            used[at] += 1
            at ^= 1
        self.end = used


def body_keys(first, last):
    return [(s, n) for s in range(SLOTS) for t in range(HALF_STEPS) for n in items_at(s, t, first, last)]


def attention_kernel(nc, x, wqkv, wout, bias, scale, consts, out):
    B, C, N = x.shape
    HID = wout.shape[0] * wout.shape[1]
    D = 64
    HEADS = HID // D
    PAIRS = HEADS // 2
    KT = C // P
    MT = C // P
    JT = N // P
    HALF = N // 2
    IT = HALF // P
    WCOLS = 2 * P
    SOFT = float(D) ** -0.5
    XS = 4
    assert PAIRS * 2 == SLOTS and JT == STEPS and N == 1024 and C == 512

    VA, VB = 4, 5
    RING_OF = {0: 0, VB: 0, VA: 1, 2: 1, 1: 2, 3: 2}

    pro = AuxCounts([(7, n) for n in PRO_ITEMS], (0, 0))
    body0 = AuxCounts(body_keys(True, False), pro.end)
    loop = AuxCounts(body_keys(False, False), body0.end)
    per_batch = (loop.end[0] - loop.start[0], loop.end[1] - loop.start[1])
    assert per_batch[0] == per_batch[1]
    LOOPS = B - 2
    bodyz = AuxCounts(body_keys(False, True), [s + LOOPS * n for s, n in zip(loop.start, per_batch)])
    epi = AuxCounts([(0, n) for n in EPI_ITEMS], bodyz.end)

    ctx = ExitStack()
    with ctx:
        def sb(name, shape, dt=F32):
            return ctx.enter_context(nc.sbuf_tensor(name, shape, dt))

        def psum(name, shape):
            return ctx.enter_context(nc.psum_tensor(name, shape, F32))

        def sem(name):
            return ctx.enter_context(nc.semaphore(name))

        x_stage = sb("x_stage", [P, XS, HALF])
        x_hi = sb("x_hi", [P, KT, N], F32R)
        x_lo = sb("x_lo", [P, KT, N], F32R)
        w_ring = sb("w_ring", [P, 3, 2, KT, WCOLS], F32R)
        wo_hi = sb("wo_hi", [P, PAIRS, C], F32R)
        wo_lo = sb("wo_lo", [P, PAIRS, C], F32R)
        q_hl = sb("q_hl", [P, 2, 2, HALF], F32R)
        q_hm = sb("q_hm", [P, 2, 2, HALF], F32R)
        k_hh = sb("k_hh", [P, 2, 2, N], F32R)
        k_l1 = sb("k_l1", [P, 2, 2, N], F32R)
        v_sb = sb("v_sb", [P, 2, JT, WCOLS])
        probs = sb("probs", [P, STEPS // 2, 2, HALF])
        prob_sum = sb("prob_sum", [P, 2, HALF])
        o_norm = sb("o_norm", [P, HALF])
        o_hi = sb("o_hi", [P, HALF], F32R)
        o_lo = sb("o_lo", [P, HALF], F32R)
        y_sb = sb("y_sb", [P, 2, MT, HALF])
        inv_sum = sb("inv_sum", [P, HALF])
        sq_a = sb("sq_a", [P, HALF])
        sq_b = sb("sq_b", [P, HALF])
        rms_a = sb("rms_a", [P, HALF])
        rms_b = sb("rms_b", [P, HALF])
        resid = sb("resid", [P, MT, HALF])
        neg_ident = sb("neg_ident", [P, P])
        tile_mask = sb("tile_mask", [IT, HALF])
        ones_d = sb("ones_d", [P, D])
        ones_c = sb("ones_c", [P, P])
        bias_sb = sb("bias_sb", [P, MT])
        scale_sb = sb("scale_sb", [P, MT])
        maxima = sb("maxima", [P, 2 * IT])

        y_flat = y_sb[:].rearrange("p h m n -> p (h m n)")
        p_flat = probs[:].rearrange("p a e n -> p (a e n)")
        W1 = KT * WCOLS
        raw_at = {0: y_flat[:, 0:W1], VA: y_flat[:, W1:2 * W1], 1: p_flat[:, 2 * W1:3 * W1],
                  2: p_flat[:, 3 * W1:4 * W1], 3: y_flat[:, 0:W1], VB: y_flat[:, W1:2 * W1]}
        raw_wo = p_flat[:, 0:2 * W1]
        spill = y_flat[:, 2 * W1:4 * W1].bitcast(F32R)

        w_split = nc.dram_tensor("w_split", [6, P, 2 * W1], F32, kind="Internal").ap()

        score = [psum(f"score{e}", [P, HALF]) for e in range(2)]
        pv = [psum(f"pv{h}", [P, HALF]) for h in range(2)]
        aux = [psum(f"aux{i}", [P, 2 * HALF]) for i in range(2)]

        aux_full = [sem("aux_full0"), sem("aux_full1")]
        aux_free = [sem("aux_free0"), sem("aux_free1")]
        score_ready = sem("score_ready")
        prob_ready = sem("prob_ready")
        pv_done = sem("pv_done")
        prob_added = sem("prob_added")
        q_hi_ready = sem("q_hi_ready")
        k_hi_ready = sem("k_hi_ready")
        onorm_ready = sem("onorm_ready")
        ohi_ready = sem("ohi_ready")
        olo_ready = sem("olo_ready")
        sq_made = sem("sq_made")
        sq_added = sem("sq_added")
        ms_ready = sem("ms_ready")
        inv_ms_ready = sem("inv_ms_ready")
        rinv_ready = sem("rinv_ready")
        y_scaled = sem("y_scaled")
        resid_added = sem("resid_added")
        resid_loaded = [sem(f"resid_loaded{i}") for i in range(MT)]
        out_stored = sem("out_stored")
        x_loaded = [sem(f"x_loaded{i}") for i in range(XS)]
        xhi_ready = sem("xhi_ready")
        x_split = [sem("x_split0"), sem("x_split1")]
        w_loaded = [sem(f"w_loaded{i}") for i in range(3)]
        raw_loaded = {c: sem(f"raw_loaded{c}") for c in range(6)}
        raw_wo_loaded = sem("raw_wo_loaded")
        const_loaded = sem("const_loaded")
        const_set = sem("const_set")
        w_hi_set = sem("w_hi_set")
        w_set = sem("w_set")
        spill_hi_set = sem("spill_hi_set")
        spill_set = sem("spill_set")
        wo_set = sem("wo_set")
        spilled = sem("spilled")
        spilled_t = sem("spilled_t")

        x_v = x.rearrange("b (k p) n -> b k p n", p=P)
        out_v = out.rearrange("b (k p) n -> b k p n", p=P)

        def aux_counts(plan, b, key):
            at, n = plan.place[key]
            if plan is loop:
                return at, (b - 1) * per_batch[at] + plan.start[at] + n
            return at, plan.start[at] + n

        class Body:

            def __init__(self, plan, b, first, last):
                self.plan, self.b, self.first, self.last = plan, b, first, last

            def at(self, slot, name):
                return aux_counts(self.plan, self.b, (slot, name))

            def full(self, eng, slot, name):
                at, n = self.at(slot, name)
                eng.wait_ge(aux_full[at], n + 1)
                return at

            def consumed(self, eng, slot, name):
                at, n = self.at(slot, name)
                eng.wait_ge(aux_free[at], n + 1)

        def split_x(eng, c, n):
            eng.wait_ge(xhi_ready, 2 * KT * n + c + 1)
            cols = slice((c % 2) * HALF, (c % 2 + 1) * HALF)
            eng.tensor_tensor(x_lo[:, c // 2, cols], x_stage[:, c % XS, :],
                              x_hi[:, c // 2, cols].bitcast(F32), ALU.subtract
                              ).then_inc(x_split[c % 2], 1)

        def run_bodies(eng, one):
            one(Body(body0, 0, True, False))
            with eng.Fori(1, 1 + LOOPS) as b:
                one(Body(loop, b, False, False))
            one(Body(bodyz, B - 1, False, True))

        def earlier_at(body, slot, name):
            if body.plan is body0:
                plan, start = pro, pro.start
            elif body.plan is epi:
                plan, start = bodyz, bodyz.start
            else:
                at, n = loop.place[(slot, name)]
                base = body.plan.start[at] + ((body.b - 1) * per_batch[at] if body.plan is loop else 0)
                return at, base - (per_batch[at] - n)
            at, n = plan.place[(slot, name)]
            return at, start[at] + n

        def wait_items(eng, what, places):
            for at, n in dict(places).items():
                eng.wait_ge(what[at], n + 1)

        block = ctx.enter_context(nc.Block())

        @block.sync
        def _(sp):
            def load_x(b, c):
                sp.dma_start(x_stage[:, c % XS, :],
                             x_v[b, c // 2, :, (c % 2) * HALF:(c % 2 + 1) * HALF]
                             ).then_inc(x_loaded[c % XS], 16)

            sp.dma_start(raw_at[0], wqkv[0]).then_inc(raw_loaded[0], 16)
            for c in range(XS):
                load_x(0, c)
            sp.dma_start(neg_ident[:], consts[:, 0:P]).then_inc(const_loaded, 16)
            sp.dma_start(tile_mask[:], consts[0:IT, P:P + HALF]).then_inc(const_loaded, 16)
            sp.dma_start(bias_sb[:], bias).then_inc(const_loaded, 16)
            sp.dma_start(scale_sb[:], scale).then_inc(const_loaded, 16)
            sp.dma_start(raw_at[VA], wqkv[VA]).then_inc(raw_loaded[VA], 16)
            for c in range(XS, 2 * KT):
                sp.wait_ge(x_split[c % 2], (c - XS) // 2 + 1)
                load_x(0, c)
            sp.dma_start(raw_at[1], wqkv[1]).then_inc(raw_loaded[1], 16)
            sp.dma_start(raw_wo, wout.rearrange("p a n -> p (a n)")).then_inc(raw_wo_loaded, 16)
            sp.dma_start(raw_at[2], wqkv[2]).then_inc(raw_loaded[2], 16)
            for n, c in enumerate((0, VA, 1)):
                sp.wait_ge(w_set, n + 1)
                sp.dma_start(w_split[c], w_ring[:, RING_OF[c]].rearrange("p h k n -> p (h k n)").bitcast(F32)
                             ).then_inc(spilled, 16)
                if c != 1:
                    late = {0: 3, VA: VB}[c]
                    sp.dma_start(raw_at[late], wqkv[late]).then_inc(raw_loaded[late], 16)
            for n, c in enumerate((2, 3, VB)):
                sp.wait_ge(spill_set, n + 1)
                sp.dma_start(w_split[c], spill.bitcast(F32)).then_inc(spilled_t, 16)
            sp.wait_ge(spilled, 48)
            sp.wait_ge(spilled_t, 48)

            def load_w(c):
                ring = RING_OF[c]
                sp.dma_start(w_ring[:, ring].rearrange("p h k n -> p (h k n)").bitcast(F32), w_split[c]
                             ).then_inc(w_loaded[ring], 16)

            def finish_half(b, half, body_after=None):
                done = b * 2 + half
                cols = slice(half * HALF, (half + 1) * HALF)
                if half == 1 or body_after is None:
                    sp.wait_ge(out_stored, 16 * MT * done)
                for m in range(MT):
                    sp.dma_start(resid[:, m, :], x_v[b, m, :, cols]).then_inc(resid_loaded[m], 16)
                for m in range(MT):
                    sp.wait_ge(resid_added, 4 * done + m + 1)
                    sp.dma_start(out_v[b, m, :, cols], resid[:, m, :]).then_inc(out_stored, 16)

            def one(body):
                b = body.b
                wait_items(sp, aux_full, [earlier_at(body, 7, "V1")])
                load_w(2)
                body.full(sp, 0, "Q")
                load_w(VB)
                if not body.first:
                    finish_half(b - 1, 0, body)
                body.full(sp, 2, "Q")
                load_w(3)
                if not body.first:
                    finish_half(b - 1, 1, body)
                if not body.last:
                    body.full(sp, 2, "V1")
                    load_w(0)
                    body.full(sp, 4, "Q")
                    load_w(VA)
                    for c in range(XS - 1):
                        if c < 2:
                            sp.wait_ge(x_split[c], KT * (b + 1))
                        load_x(b + 1, c)
                    if not body.first:
                        sp.wait_ge(out_stored, 16 * MT * 2 * b)
                    load_x(b + 1, XS - 1)
                    body.full(sp, 6, "Q")
                    load_w(1)
                    for c in range(XS, 2 * KT):
                        sp.wait_ge(x_split[c % 2], KT * (b + 1) + (c - XS) // 2 + 1)
                        load_x(b + 1, c)

            run_bodies(sp, one)
            finish_half(B - 1, 0)
            finish_half(B - 1, 1)
            sp.wait_ge(out_stored, 16 * MT * 2 * B)

        @block.tensor
        def _(pe):
            def claim(body, slot, name, after=()):
                at, n = body.at(slot, name)
                if not (body.plan is pro and n == 0):
                    pe.wait_ge(aux_free[at], n)
                wait_items(pe, aux_free, [(a, i) for a, i in (body.at(*key) for key in after) if a != at])
                return at

            def wait_w(body, chunk, next_batch):
                ring = RING_OF[chunk]
                if body.plan is pro:
                    pe.wait_ge(w_set, {0: 1, VA: 2}[chunk])
                elif chunk in (0, 1, VA):
                    if body.first and not next_batch:
                        pe.wait_ge(w_set, 3)
                    else:
                        pe.wait_ge(w_loaded[ring], 16 * (2 * (body.b + (1 if next_batch else 0))))
                else:
                    pe.wait_ge(w_loaded[ring], 16 * (2 * body.b + 1))

            def project(out_ap, w, cols, xcols):
                n = 0
                for k in range(KT):
                    for wp, xp in ((0, x_hi), (1, x_hi), (0, x_lo)):
                        last = pe.matmul(out_ap, w[:, wp, k, cols], xp[:, k, xcols],
                                         start=(n == 0), stop=(n == 3 * KT - 1))
                        n += 1
                return last

            def item(body, slot, name):
                nslot = (slot + 1) % SLOTS
                npair, nhalf = divmod(nslot, 2)
                nb = slot == 7
                if name == "Q":
                    at = claim(body, slot, name)
                    if slot == 7:
                        for by in x_split:
                            pe.wait_ge(by, KT * (body.b + 2))
                    wait_w(body, npair, nb)
                    project(aux[at][:, 0:HALF], w_ring[:, RING_OF[npair]], slice(0, P),
                            slice(nhalf * HALF, (nhalf + 1) * HALF)).then_inc(aux_full[at], 1)
                elif name == "K":
                    kpair = (slot // 2 + 1) % PAIRS
                    at = claim(body, slot, name)
                    wait_w(body, kpair, nb)
                    for h in range(2):
                        last = project(aux[at][:, h * HALF:(h + 1) * HALF],
                                       w_ring[:, RING_OF[kpair]], slice(P, 2 * P),
                                       slice(h * HALF, (h + 1) * HALF))
                    last.then_inc(aux_full[at], 1)
                elif name in ("V0", "V1"):
                    chunk = VA if nb else VB
                    at = claim(body, slot, name)
                    wait_w(body, chunk, nb)
                    w = w_ring[:, RING_OF[chunk]]
                    for i in range(JT // 2):
                        jt = int(name[1]) * (JT // 2) + i
                        n = 0
                        for k in range(KT):
                            for wp, xp in ((0, x_hi), (1, x_hi), (0, x_lo)):
                                last = pe.matmul(aux[at][:, i * WCOLS:(i + 1) * WCOLS],
                                                 xp[:, k, jt * P:(jt + 1) * P], w[:, wp, k, :],
                                                 start=(n == 0), stop=(n == 3 * KT - 1))
                                n += 1
                    last.then_inc(aux_full[at], 1)
                elif name[0] == "M":
                    e, it = divmod(int(name[1]), IT)
                    after = []
                    if name == "M0":
                        after = [(slot, "Q")]
                        if nslot == 0:
                            after = [(slot, "Q"), (slot, "K")]
                        elif nhalf == 0:
                            after = [(slot - 1, "K"), (slot, "Q")]
                    at = claim(body, slot, name, after)
                    for h in range(2):
                        last = pe.matmul(aux[at][:, h * HALF:(h + 1) * HALF],
                                         q_hl[:, nhalf, e, it * P:(it + 1) * P],
                                         k_hh[:, npair % 2, e, h * HALF:(h + 1) * HALF],
                                         start=True, stop=True)
                    last.then_inc(aux_full[at], 1)
                elif name == "T":
                    at = claim(body, slot, name, [(slot, "M6"), (slot, "M7")])
                    for e in range(2):
                        last = pe.matmul(aux[at][0:IT, e * P:(e + 1) * P],
                                         maxima[:, e * IT:(e + 1) * IT], neg_ident[:],
                                         start=True, stop=True)
                    last.then_inc(aux_full[at], 1)
                elif name == "L":
                    done = body.b * SLOTS + slot
                    at = claim(body, slot, name)
                    pe.wait_ge(prob_added, 14 * done)
                    for e in range(2):
                        last = pe.matmul(aux[at][e * D:(e + 1) * D, 0:HALF], ones_d[:],
                                         prob_sum[:, e, :], start=True, stop=True)
                    last.then_inc(aux_full[at], 1)
                elif name in ("O0", "O1"):
                    done = body.b * SLOTS + slot
                    pair = (slot - 1) % SLOTS // 2
                    at = claim(body, slot, name)
                    if name == "O0":
                        pe.wait_ge(olo_ready, done)
                        if body.first and slot == 1:
                            pe.wait_ge(wo_set, 1)
                    for i in range(2):
                        m = 2 * int(name[1]) + i
                        for n, (w, o) in enumerate(((wo_hi, o_hi), (wo_lo, o_hi), (wo_hi, o_lo))):
                            last = pe.matmul(aux[at][:, i * HALF:(i + 1) * HALF],
                                             w[:, pair, m * P:(m + 1) * P], o[:],
                                             start=(n == 0), stop=(n == 2))
                    last.then_inc(aux_full[at], 1)
                else:
                    half = int(name[1]) if name != "R" else slot
                    batch = body.b if name in ("R0", "R1") else body.b - 1
                    at = claim(body, slot, name)
                    pe.wait_ge(sq_added, 3 * (2 * batch + half + 1))
                    pe.matmul(aux[at][:, 0:HALF], ones_c[:], sq_a[:], start=True, stop=True
                              ).then_inc(aux_full[at], 1)

            def scores(body, slot, j):
                pair, half = divmod(slot, 2)
                for e in range(2):
                    n = body.b * 128 + slot * 16 + 2 * j + e
                    if not (body.first and slot == 0 and j == 0):
                        pe.wait_ge(prob_ready, n - 1)
                    keys = slice(j * P, (j + 1) * P)
                    pe.matmul(score[e][:], k_hh[:, pair % 2, e, keys], q_hl[:, half, e, :],
                              start=True, stop=False)
                    pe.matmul(score[e][:], k_l1[0:D + IT, pair % 2, e, keys],
                              q_hm[0:D + IT, half, e, :], start=False, stop=True
                              ).then_inc(score_ready, 1)

            def values(body, slot, j, back):
                pair, half = divmod(slot, 2)
                b = body.b - 1 if back else body.b
                for e in range(2):
                    n = b * 128 + slot * 16 + 2 * j + e
                    pe.wait_ge(prob_ready, n + 1)
                    if j == 0 and e == 0 and not (body.first and slot < 2):
                        pe.wait_ge(onorm_ready, b * SLOTS + slot - 1)
                    pe.matmul(pv[half][e * D:(e + 1) * D, :],
                              v_sb[:, pair // 2, j, (pair % 2) * P + e * D:(pair % 2) * P + (e + 1) * D],
                              probs[:, j % 4, e, :], start=(j == 0), stop=(j == STEPS - 1)
                              ).then_inc(pv_done, 1)

            def one(body):
                for slot in range(SLOTS):
                    if slot == 0:
                        wait_items(pe, aux_free, [earlier_at(body, 7, n) for n in ("V0", "V1", "T")])
                    elif slot == 4:
                        wait_items(pe, aux_free, [body.at(1, "V0"), body.at(2, "V1"), body.at(3, "T")])
                    else:
                        body.consumed(pe, slot - 1, "T")
                    for t in range(HALF_STEPS):
                        j = t // 2
                        if t % 2 == 0:
                            scores(body, slot, j)
                        elif j > 0:
                            values(body, slot, j - 1, False)
                        elif slot > 0:
                            values(body, slot - 1, STEPS - 1, False)
                        elif not body.first:
                            values(body, SLOTS - 1, STEPS - 1, True)
                        for name in items_at(slot, t, body.first, body.last):
                            item(body, slot, name)

            pe.wait_ge(const_loaded, 64)
            pe.wait_ge(const_set, 3)
            start = Body(pro, -1, True, True)
            for name in PRO_ITEMS:
                item(start, 7, name)
            run_bodies(pe, one)
            end = Body(epi, B, False, True)
            values(end, SLOTS - 1, STEPS - 1, True)
            for name in ("L", "O0", "O1"):
                item(end, 0, name)
            last = Body(epi, B - 1, False, True)
            item(last, 0, "R0")
            item(last, 0, "R1")

        @block.scalar
        def _(act):
            def exponentials(body, slot, j):
                for e in range(2):
                    n = body.b * 128 + slot * 16 + 2 * j + e
                    act.wait_ge(score_ready, n + 1)
                    if not (body.first and slot == 0 and j < 4):
                        act.wait_ge(pv_done, n - 7)
                        base = (body.b * SLOTS + slot) * 14
                        added = base + (2 * max(j - 5, 0) + e + 1 if j >= 4 else 2 * (j + 3) + e + 1 - 14)
                        act.wait_ge(prob_added, added)
                    act.activation(probs[:, j % 4, e, :], score[e][:], ACT.Exp, scale=SOFT
                                   ).then_inc(prob_ready, 1)

            def item(body, slot, name):
                nslot = (slot + 1) % SLOTS
                npair, nhalf = divmod(nslot, 2)
                if name == "Q":
                    at = body.full(act, slot, name)
                    for e in range(2):
                        src = aux[at][e * D:(e + 1) * D, 0:HALF]
                        for dst in (q_hl[0:D, nhalf, e, :], q_hm[0:D, nhalf, e, :]):
                            act.activation(dst, src, ACT.Copy).then_inc(q_hi_ready, 1)
                elif name == "K":
                    kpair = (slot // 2 + 1) % PAIRS
                    at = body.full(act, slot, name)
                    for e in range(2):
                        rows = slice(e * D, (e + 1) * D)
                        act.activation(k_hh[rows, kpair % 2, e, :], aux[at][rows, :], ACT.Copy
                                       ).then_inc(k_hi_ready, 1)
                elif name in ("V0", "V1"):
                    at = body.full(act, slot, name)
                    j0 = int(name[1]) * (JT // 2)
                    act.activation(v_sb[:, 0 if slot == 7 else 1, j0:j0 + JT // 2, :],
                                   aux[at][:].rearrange("p (j n) -> p j n", n=WCOLS), ACT.Copy
                                   ).then_inc(aux_free[at], 1)
                elif name in ("O0", "O1") and slot in (1, 2):
                    at = body.full(act, slot, name)
                    half = slot - 1
                    if name == "O0" and not body.first:
                        act.wait_ge(resid_added, 4 * (2 * (body.b - 1) + half + 1))
                    if name == "O0" and body.first and half == 0:
                        act.wait_ge(spilled_t, 48)
                    for i in range(2):
                        m = 2 * int(name[1]) + i
                        ins = act.activation(y_sb[:, half, m, :], aux[at][:, i * HALF:(i + 1) * HALF],
                                             ACT.Identity, bias=bias_sb[:, m:m + 1])
                    ins.then_inc(aux_free[at], 1)

            def split_output_high(done):
                act.wait_ge(onorm_ready, done)
                act.activation(o_hi[:], o_norm[:], ACT.Copy).then_inc(ohi_ready, 1)

            def square(body, half, m):
                done = 2 * (body.b - 1) + half
                if m == 0 and half == 0:
                    wait_items(act, aux_free, [earlier_at(body, 7, n) for n in ("O0", "O1")])
                elif m == 0:
                    if body.plan is epi:
                        Body(epi, B - 1, False, True).full(act, 0, "R0")
                    else:
                        body.full(act, 0, "R")
                    wait_items(act, aux_free, [body.at(0, n) for n in ("O0", "O1")])
                elif m >= 2:
                    act.wait_ge(sq_added, 3 * done + m - 1)
                act.activation((sq_a if m == 0 else sq_b)[:], y_sb[:, half, m, :], ACT.Square
                               ).then_inc(sq_made, 1)

            def root(done):
                act.wait_ge(inv_ms_ready, done + 1)
                act.activation(rms_a[:], rms_b[:], ACT.Sqrt).then_inc(rinv_ready, 1)

            def split_x(c, n):
                act.wait_ge(x_loaded[c % XS], 16 * (n * 2 * KT // XS + c // XS + 1))
                act.activation(x_hi[:, c // 2, (c % 2) * HALF:(c % 2 + 1) * HALF],
                               x_stage[:, c % XS, :], ACT.Copy).then_inc(xhi_ready, 1)

            def one(body):
                for slot in range(SLOTS):
                    for t in range(HALF_STEPS):
                        if t % 2 == 0:
                            exponentials(body, slot, t // 2)
                        if t == 3 and slot in (1, 2) and not body.first:
                            root(2 * (body.b - 1) + slot - 1)
                        for name in items_at(slot, t, body.first, body.last):
                            item(body, slot, name)
                        if t == 6 and not (body.first and slot == 0):
                            split_output_high(body.b * SLOTS + slot)
                        if t in SQUARE_AT and slot in (0, 1) and not body.first:
                            square(body, slot, SQUARE_AT.index(t))
                        if slot == 6 and not body.last and t in SPLIT_AT:
                            if t == SPLIT_AT[0]:
                                body.full(act, 6, "Q")
                            split_x(SPLIT_AT.index(t), body.b + 1)

            for c in range(2 * KT):
                split_x(c, 0)
            start = Body(pro, -1, True, True)
            act.wait_ge(const_loaded, 64)
            for name in PRO_ITEMS:
                item(start, 7, name)
            act.wait_ge(w_set, 3)
            act.wait_ge(wo_set, 1)
            act.wait_ge(spill_set, 1)
            run_bodies(act, one)
            end = Body(epi, B, False, True)
            split_output_high(B * SLOTS)
            for half in range(2):
                for m in range(MT):
                    square(end, half, m)
                root(2 * (B - 1) + half)

        @block.vector
        def _(dve):
            def item(body, slot, name):
                nslot = (slot + 1) % SLOTS
                npair, nhalf = divmod(nslot, 2)
                if name == "Q":
                    at = body.full(dve, slot, name)
                    before = SLOTS * body.b + slot + 1
                    for e in range(2):
                        dve.wait_ge(q_hi_ready, 4 * before + 2 * e + 2)
                        ins = dve.tensor_tensor(q_hl[D:2 * D, nhalf, e, :],
                                                aux[at][e * D:(e + 1) * D, 0:HALF],
                                                q_hl[0:D, nhalf, e, :].bitcast(F32), ALU.subtract)
                    ins.then_inc(aux_free[at], 1)
                elif name == "K":
                    at = body.full(dve, slot, name)
                    before = PAIRS * body.b + (slot + 1) // 2 + (slot != 7)
                    kp = (slot // 2 + 1) % PAIRS % 2
                    for e in range(2):
                        rows, others = slice(e * D, (e + 1) * D), slice((1 - e) * D, (2 - e) * D)
                        dve.wait_ge(k_hi_ready, 2 * before + e + 1)
                        dve.tensor_copy(k_hh[others, kp, e, :], k_hh[rows, kp, e, :].bitcast(F32))
                        ins = dve.tensor_tensor(k_l1[0:D, kp, e, :], aux[at][rows, :],
                                                k_hh[rows, kp, e, :].bitcast(F32), ALU.subtract)
                    ins.then_inc(aux_free[at], 1)
                elif name[0] == "M":
                    at = body.full(dve, slot, name)
                    n = int(name[1])
                    dve.tensor_reduce(maxima[:, n:n + 1], aux[at][:], AX_X, ALU.max
                                      ).then_inc(aux_free[at], 1)
                elif name == "T":
                    at = body.full(dve, slot, name)
                    for e in range(2):
                        ins = dve.tensor_tensor(
                            q_hm[D:D + IT, nhalf, e, :].rearrange("t (i n) -> t i n", i=IT),
                            aux[at][0:IT, e * P:(e + 1) * P].unsqueeze(1).to_broadcast([IT, IT, P]),
                            tile_mask[:].rearrange("t (i n) -> t i n", i=IT), ALU.mult)
                    ins.then_inc(aux_free[at], 1)
                elif name == "L":
                    at = body.full(dve, slot, name)
                    dve.reciprocal(inv_sum[:], aux[at][:, 0:HALF]).then_inc(aux_free[at], 1)
                elif name in ("O0", "O1") and slot not in (1, 2):
                    half, m = (slot - 1) % 2, 2 * int(name[1])
                    at = body.full(dve, slot, name)
                    if slot in (3, 4):
                        body.consumed(dve, slot - 2, name)
                    elif slot == 0:
                        wait_items(dve, aux_free, [earlier_at(body, 6, name)])
                    else:
                        body.consumed(dve, slot - 2, name)
                    y = y_sb[:, half, m:m + 2, :].rearrange("p m n -> p (m n)")
                    dve.tensor_tensor(y, y, aux[at][:], ALU.add).then_inc(aux_free[at], 1)
                elif name[0] == "R":
                    half = int(name[1]) if name != "R" else slot
                    batch = body.b if name in ("R0", "R1") else body.b - 1
                    done = 2 * batch + half
                    at = body.full(dve, slot, name)
                    if name == "R1":
                        dve.wait_ge(y_scaled, 4 * done)
                    dve.tensor_scalar(rms_a[:], aux[at][:, 0:HALF], SOFT, None, ALU.add
                                      ).then_inc(aux_free[at], 1)

            def invert(body, slot, name):
                body.consumed(dve, slot, name)
                dve.reciprocal(rms_b[:], rms_a[:]).then_inc(inv_ms_ready, 1)

            def normalise(body, slot):
                done = body.b * SLOTS + slot
                body.consumed(dve, slot, "L")
                dve.wait_ge(pv_done, 16 * done)
                dve.tensor_tensor(o_norm[:], inv_sum[:], pv[(slot - 1) % 2][:], ALU.mult
                                  ).then_inc(onorm_ready, 1)

            def split_output_low(done):
                dve.wait_ge(ohi_ready, done)
                dve.tensor_tensor(o_lo[:], o_norm[:], o_hi[:].bitcast(F32), ALU.subtract
                                  ).then_inc(olo_ready, 1)

            def add_square(done, m):
                dve.wait_ge(sq_made, 4 * done + m + 1)
                if m > 1:
                    dve.wait_ge(sq_added, 3 * done + m - 1)
                dve.tensor_tensor(sq_a[:], sq_a[:], sq_b[:], ALU.add).then_inc(sq_added, 1)

            def scale_y(done, half):
                dve.wait_ge(rinv_ready, done + 1)
                for m in range(MT):
                    dve.scalar_tensor_tensor(out=y_sb[:, half, m, :], in0=y_sb[:, half, m, :],
                                             scalar=scale_sb[:, m:m + 1], in1=rms_a[:],
                                             op0=ALU.mult, op1=ALU.mult).then_inc(y_scaled, 1)

            def split_w(n, c):
                dve.wait_ge(raw_loaded[c], 16)
                ring = w_ring[:, RING_OF[c]].rearrange("p h k n -> p h (k n)")
                dve.tensor_copy(ring[:, 0], raw_at[c]).then_inc(w_hi_set, 1)
                dve.wait_ge(w_hi_set, n + 1)
                dve.tensor_tensor(ring[:, 1], raw_at[c], ring[:, 0].bitcast(F32), ALU.subtract
                                  ).then_inc(w_set, 1)

            def one(body):
                for slot in range(SLOTS):
                    for t in range(HALF_STEPS):
                        for name in items_at(slot, t, body.first, body.last):
                            item(body, slot, name)
                        if t == 0 and slot in (1, 2) and not body.first:
                            invert(body, slot - 1, "R")
                        if t == 5 and not (body.first and slot == 0):
                            normalise(body, slot)
                        if t - 1 in SQUARE_AT[1:] and slot in (0, 1) and not body.first:
                            add_square(2 * (body.b - 1) + slot, SQUARE_AT.index(t - 1))
                        if t == 7 and not (body.first and slot == 0):
                            split_output_low(body.b * SLOTS + slot)
                        if t == 3 and slot in (1, 2) and not body.first:
                            scale_y(2 * (body.b - 1) + slot - 1, slot - 1)
                        if slot == 6 and not body.last and t in SPLIT_AT[0::2]:
                            split_x(dve, SPLIT_AT.index(t), body.b + 1)

            dve.memset(ones_d[:], 1.0).then_inc(const_set, 1)
            dve.memset(ones_c[:], 1.0 / C).then_inc(const_set, 1)
            dve.memset(k_l1[D:D + IT].rearrange("p a e n -> p (a e n)").bitcast(F32), 1.0
                       ).then_inc(const_set, 1)
            split_w(0, 0)
            for c in range(0, 2 * KT, 2):
                split_x(dve, c, 0)
                if c == 2:
                    split_w(1, VA)
            split_w(2, 1)
            dve.wait_ge(const_loaded, 64)
            start = Body(pro, -1, True, True)
            for name in PRO_ITEMS:
                item(start, 7, name)
            run_bodies(dve, one)
            end = Body(epi, B, False, True)
            item(end, 0, "L")
            normalise(end, 0)
            split_output_low(B * SLOTS)
            for name in ("O0", "O1"):
                item(end, 0, name)
            last = Body(epi, B - 1, False, True)
            for half in range(2):
                for m in range(1, MT):
                    add_square(2 * (B - 1) + half, m)
                item(last, 0, f"R{half}")
                invert(last, 0, f"R{half}")
                scale_y(2 * (B - 1) + half, half)

        @block.gpsimd
        def _(pool):
            def add_probs(body, slot, j):
                base = (body.b * SLOTS + slot) * 14
                for e in range(2):
                    n = body.b * 128 + slot * 16 + 2 * j + e
                    pool.wait_ge(prob_ready, n + 1)
                    if j == 1:
                        if e == 0 and not (body.first and slot == 0):
                            body.full(pool, slot, "L")
                        pool.tensor_tensor(prob_sum[:, e, :], probs[:, 0, e, :], probs[:, 1, e, :],
                                           ALU.add).then_inc(prob_added, 1)
                    else:
                        pool.wait_ge(prob_added, base + 2 * (j - 2) + e + 1)
                        pool.tensor_tensor(prob_sum[:, e, :], prob_sum[:, e, :], probs[:, j % 4, e, :],
                                           ALU.add).then_inc(prob_added, 1)

            def add_resid(done, half):
                for m in range(MT):
                    pool.wait_ge(y_scaled, 4 * done + m + 1)
                    pool.wait_ge(resid_loaded[m], 16 * (done + 1))
                    pool.tensor_tensor(resid[:, m, :], resid[:, m, :], y_sb[:, half, m, :],
                                       ALU.add).then_inc(resid_added, 1)

            def one(body):
                for slot in range(SLOTS):
                    for j in range(STEPS):
                        if j:
                            add_probs(body, slot, j)
                        if slot == 6 and not body.last:
                            for c in (1, 3, 5, 7):
                                if SPLIT_AT[c] // 2 == j:
                                    split_x(pool, c, body.b + 1)
                        if body.first:
                            continue
                        if j == 3 and slot in (1, 2):
                            add_resid(2 * (body.b - 1) + slot - 1, slot - 1)

            for c in range(1, 2 * KT, 2):
                split_x(pool, c, 0)
            pool.wait_ge(raw_wo_loaded, 16)
            pool.tensor_copy(wo_hi[:].rearrange("p a n -> p (a n)"), raw_wo).then_inc(spill_hi_set, 1)
            pool.wait_ge(spill_hi_set, 1)
            pool.tensor_tensor(wo_lo[:].rearrange("p a n -> p (a n)"), raw_wo,
                               wo_hi[:].rearrange("p a n -> p (a n)").bitcast(F32), ALU.subtract
                               ).then_inc(wo_set, 1)
            for n, c in enumerate((2, 3, VB)):
                pool.wait_ge(raw_loaded[c], 16)
                if n:
                    pool.wait_ge(spilled_t, 16 * n)
                pool.tensor_copy(spill[:, 0:W1], raw_at[c]).then_inc(spill_hi_set, 1)
                pool.wait_ge(spill_hi_set, n + 2)
                pool.tensor_tensor(spill[:, W1:2 * W1], raw_at[c], spill[:, 0:W1].bitcast(F32),
                                   ALU.subtract).then_inc(spill_set, 1)
            run_bodies(pool, one)
            for half in range(2):
                add_resid(2 * (B - 1) + half, half)


def kernel(x, L0_conv_w_qkv, L0_conv_w_out, L0_conv_b_out, L0_conv_rms_scale):
    import concourse.bacc as bacc
    from concourse.bass_utils import run_bass_kernel_spmd

    x = np.ascontiguousarray(x)
    b, c, h, w = x.shape
    w_qkv, w_out = np.asarray(L0_conv_w_qkv), np.asarray(L0_conv_w_out)
    hid = w_out.shape[1]
    pairs = hid // P

    def chunk(rows):
        a = w_qkv[rows].reshape(len(rows), c // P, P)
        return a.transpose(2, 1, 0).reshape(P, -1)

    chunks = [chunk(np.r_[p * P:(p + 1) * P, hid + p * P:hid + (p + 1) * P]) for p in range(pairs)]
    chunks += [chunk(np.r_[2 * hid + s * 2 * P:2 * hid + (s + 1) * 2 * P]) for s in range(2)]
    consts = np.zeros((P, P + h * w // 2), np.float32)
    consts[:, 0:P] = -np.eye(P, dtype=np.float32)
    for t in range(h * w // 2 // P):
        consts[t, P + t * P:P + (t + 1) * P] = 1.0
    arrays = {
        "x": x.reshape(b, c, h * w),
        "wqkv": np.ascontiguousarray(np.stack(chunks)),
        "wout": np.ascontiguousarray(w_out.T.reshape(pairs, P, c).transpose(1, 0, 2)),
        "bias": np.ascontiguousarray(np.asarray(L0_conv_b_out).reshape(c // P, P).T),
        "scale": np.ascontiguousarray(np.asarray(L0_conv_rms_scale).reshape(c // P, P).T),
        "consts": consts,
    }
    nc = bacc.Bacc("TRN2", target_bir_lowering=False, num_devices=1)
    args = [nc.dram_tensor(n, a.shape, mybir.dt.from_np(a.dtype), kind="ExternalInput").ap()
            for n, a in arrays.items()]
    out = nc.dram_tensor("out", (b, c, h * w), F32, kind="ExternalOutput").ap()
    attention_kernel(nc, *args, out)
    r = run_bass_kernel_spmd(nc, [arrays], core_ids=[0])
    return r.results[0]["out"].reshape(b, c, h, w)
```

```python
from contextlib import ExitStack

import numpy as np

import concourse.bass as bass
from concourse import mybir

F32 = mybir.dt.float32
F32R = mybir.dt.float32r
ACT = mybir.ActivationFunctionType
ALU = mybir.AluOpType
AX_X = mybir.AxisListType.X

P = 128

SLOTS, STEPS = 8, 8
HALF_STEPS = 2 * STEPS
SUMS_AT = 1
VALUES_AT = 3
MAXIMA_AT = [(4, 5, 6, 7, 8, 9, 10, 11)] * SLOTS
MAXIMA_AT[6] = (4, 5, 6, 7, 8, 9, 10, 12)
ROWS_AT = 13
OUTPUT_AT = [(12, 14)] * SLOTS
OUTPUT_AT[2] = OUTPUT_AT[4] = (13, 14)
REPEAT_AT = 12
NORMALISE_AT = 5
LOW_BY_GPSIMD = (0, 1, 3, 4, 5, 7)
OUTPUT_LOW_AT = 4
SPLIT_AT = (1, 2, 3, 4, 8, 9, 10, 12)
SQUARE_AT = (3, 6, 8, 10)
MEAN_AT = (13, 15)
INVERT_AT = ((0, 13), (2, 0))
SCALE_AT = ((0, 15), (2, 3))
RESIDUAL_AT = ((0, 0, 0, 0), (2, 2, 3, 3))


def items_at(slot, t, first, last):
    following = not (last and slot == SLOTS - 1)
    preceding = not (first and slot == 0)
    out = []
    if t == 0 and following:
        out.append("Q")
    if t == SUMS_AT and preceding:
        out.append("L")
    if following:
        out += [f"M{i}" for i, at in enumerate(MAXIMA_AT[slot]) if t == at]
        if slot == 7:
            out += {2: ["K"], 3: ["V0"], 15: ["V1"]}.get(t, [])
    if slot in (1, 2) and t == VALUES_AT:
        out.append(f"V{slot - 1}")
    if slot in (0, 1) and t == MEAN_AT[slot] and not first:
        out.append("R")
    if t == ROWS_AT and following:
        out.append("T")
    out += [f"O{i}" for i, at in enumerate(OUTPUT_AT[slot]) if t == at and preceding]
    if t == 15 and slot in (0, 2, 4):
        out.append("K")
    return out


PRO_ITEMS = ["Q", "K", "V0", "V1"] + [f"M{i}" for i in range(8)] + ["T"]
EPI_ITEMS = ["L", "O0", "O1", "R0", "R1"]


class AuxCounts:

    def __init__(self, names, start):
        self.start, self.place = list(start), {}
        used, at = list(start), (start[0] + start[1]) % 2
        for key in names:
            self.place[key] = (at, used[at] - start[at])
            used[at] += 1
            at ^= 1
        self.end = used


def body_keys(first, last):
    return [(s, n) for s in range(SLOTS) for t in range(HALF_STEPS) for n in items_at(s, t, first, last)]


def attention_kernel(nc, x, wqkv, wout, bias, scale, consts, out):
    B, C, N = x.shape
    HID = wout.shape[0] * wout.shape[1]
    D = 64
    HEADS = HID // D
    PAIRS = HEADS // 2
    KT = C // P
    MT = C // P
    JT = N // P
    HALF = N // 2
    IT = HALF // P
    WCOLS = 2 * P
    SOFT = float(D) ** -0.5
    XS = 4
    assert PAIRS * 2 == SLOTS and JT == STEPS and N == 1024 and C == 512

    VA, VB = 4, 5
    RING_OF = {0: 0, VB: 0, VA: 1, 2: 1, 1: 2, 3: 2}

    pro = AuxCounts([(7, n) for n in PRO_ITEMS], (0, 0))
    body0 = AuxCounts(body_keys(True, False), pro.end)
    loop = AuxCounts(body_keys(False, False), body0.end)
    per_batch = (loop.end[0] - loop.start[0], loop.end[1] - loop.start[1])
    assert per_batch[0] == per_batch[1]
    LOOPS = B - 2
    bodyz = AuxCounts(body_keys(False, True), [s + LOOPS * n for s, n in zip(loop.start, per_batch)])
    epi = AuxCounts([(0, n) for n in EPI_ITEMS], bodyz.end)

    ctx = ExitStack()
    with ctx:
        def sb(name, shape, dt=F32):
            return ctx.enter_context(nc.sbuf_tensor(name, shape, dt))

        def psum(name, shape):
            return ctx.enter_context(nc.psum_tensor(name, shape, F32))

        def sem(name):
            return ctx.enter_context(nc.semaphore(name))

        x_stage = sb("x_stage", [P, XS, HALF])
        x_hi = sb("x_hi", [P, KT, N], F32R)
        x_lo = sb("x_lo", [P, KT, N], F32R)
        w_ring = sb("w_ring", [P, 3, 2, KT, WCOLS], F32R)
        wo_hi = sb("wo_hi", [P, PAIRS, C], F32R)
        wo_lo = sb("wo_lo", [P, PAIRS, C], F32R)
        q_hl = sb("q_hl", [P, 2, 2, HALF], F32R)
        q_hm = sb("q_hm", [P, 2, 2, HALF], F32R)
        k_hh = sb("k_hh", [P, 2, 2, N], F32R)
        k_l1 = sb("k_l1", [P, 2, 2, N], F32R)
        v_sb = sb("v_sb", [P, 2, JT, WCOLS])
        probs = sb("probs", [P, STEPS // 2, 2, HALF])
        prob_sum = sb("prob_sum", [P, 2, HALF])
        o_norm = sb("o_norm", [P, HALF])
        o_hi = sb("o_hi", [P, HALF], F32R)
        o_lo = sb("o_lo", [P, HALF], F32R)
        y_sb = sb("y_sb", [P, 2, MT, HALF])
        inv_sum = sb("inv_sum", [P, HALF])
        sq_a = sb("sq_a", [P, HALF])
        sq_b = sb("sq_b", [P, HALF])
        rms_a = sb("rms_a", [P, HALF])
        rms_b = sb("rms_b", [P, HALF])
        resid = sb("resid", [P, MT, HALF])
        neg_ident = sb("neg_ident", [P, P])
        tile_mask = sb("tile_mask", [2 * IT, 2 * HALF], mybir.dt.bfloat16)
        ones_d = sb("ones_d", [P, D])
        ones_c = sb("ones_c", [P, P])
        bias_sb = sb("bias_sb", [P, MT])
        scale_sb = sb("scale_sb", [P, MT])
        table_back = sb("table_back", [P, 1])
        maxima = sb("maxima", [P, 2 * IT])

        y_flat = y_sb[:].rearrange("p h m n -> p (h m n)")
        p_flat = probs[:].rearrange("p a e n -> p (a e n)")
        W1 = KT * WCOLS
        raw_at = {0: y_flat[:, 0:W1], VA: y_flat[:, W1:2 * W1], 1: p_flat[:, 2 * W1:3 * W1],
                  2: p_flat[:, 3 * W1:4 * W1], 3: y_flat[:, 0:W1], VB: y_flat[:, W1:2 * W1]}
        raw_wo = p_flat[:, 0:2 * W1]
        raw_mask = resid[:].rearrange("p m n -> p (m n)")[0:2 * IT, 0:2 * HALF]
        spill = y_flat[:, 2 * W1:4 * W1].bitcast(F32R)

        w_split = nc.dram_tensor("w_split", [6, P, 2 * W1], F32, kind="Internal").ap()

        score = [psum(f"score{e}", [P, HALF]) for e in range(2)]
        pv = [psum(f"pv{h}", [P, HALF]) for h in range(2)]
        aux = [psum(f"aux{i}", [P, 2 * HALF]) for i in range(2)]

        aux_full = [sem("aux_full0"), sem("aux_full1")]
        aux_free = [sem("aux_free0"), sem("aux_free1")]
        score_ready = sem("score_ready")
        prob_ready = sem("prob_ready")
        pv_done = sem("pv_done")
        prob_added = sem("prob_added")
        q_hi_ready = sem("q_hi_ready")
        q_repeated = sem("q_repeated")
        k_hi_ready = sem("k_hi_ready")
        onorm_ready = sem("onorm_ready")
        ohi_ready = sem("ohi_ready")
        olo_ready = sem("olo_ready")
        sq_made = sem("sq_made")
        sq_added = sem("sq_added")
        inv_ms_ready = sem("inv_ms_ready")
        rinv_ready = sem("rinv_ready")
        y_scaled = sem("y_scaled")
        resid_added = sem("resid_added")
        resid_loaded = [sem(f"resid_loaded{i}") for i in range(MT)]
        out_stored = sem("out_stored")
        x_loaded = [sem(f"x_loaded{i}") for i in range(XS)]
        xhi_ready = sem("xhi_ready")
        x_split = [sem("x_split0"), sem("x_split1")]
        w_loaded = [sem(f"w_loaded{i}") for i in range(3)]
        raw_loaded = {c: sem(f"raw_loaded{c}") for c in range(6)}
        raw_wo_loaded = sem("raw_wo_loaded")
        const_loaded = sem("const_loaded")
        const_set = sem("const_set")
        mask_set = sem("mask_set")
        w_hi_set = sem("w_hi_set")
        w_set = sem("w_set")
        spill_hi_set = sem("spill_hi_set")
        spill_set = sem("spill_set")
        wo_set = sem("wo_set")
        spilled = sem("spilled")
        spilled_late = sem("spilled_late")

        x_v = x.rearrange("b (k p) n -> b k p n", p=P)
        out_v = out.rearrange("b (k p) n -> b k p n", p=P)

        def aux_counts(plan, b, key):
            at, n = plan.place[key]
            if plan is loop:
                return at, (b - 1) * per_batch[at] + plan.start[at] + n
            return at, plan.start[at] + n

        class Body:

            def __init__(self, plan, b, first, last):
                self.plan, self.b, self.first, self.last = plan, b, first, last

            def at(self, slot, name):
                return aux_counts(self.plan, self.b, (slot, name))

            def full(self, eng, slot, name):
                at, n = self.at(slot, name)
                eng.wait_ge(aux_full[at], n + 1)
                return at

            def consumed(self, eng, slot, name):
                at, n = self.at(slot, name)
                eng.wait_ge(aux_free[at], n + 1)

        def split_x(eng, c, n):
            eng.wait_ge(xhi_ready, 2 * KT * n + c + 1)
            cols = slice((c % 2) * HALF, (c % 2 + 1) * HALF)
            eng.tensor_tensor(x_lo[:, c // 2, cols], x_stage[:, c % XS, :],
                              x_hi[:, c // 2, cols].bitcast(F32), ALU.subtract
                              ).then_inc(x_split[c % 2], 1)

        def split_output_low(eng, done):
            eng.wait_ge(ohi_ready, done)
            eng.tensor_tensor(o_lo[:], o_norm[:], o_hi[:].bitcast(F32), ALU.subtract
                              ).then_inc(olo_ready, 1)

        def run_bodies(eng, one):
            one(Body(body0, 0, True, False))
            with eng.Fori(1, 1 + LOOPS) as b:
                one(Body(loop, b, False, False))
            one(Body(bodyz, B - 1, False, True))

        def earlier_at(body, slot, name):
            if body.plan is body0:
                plan, start = pro, pro.start
            elif body.plan is epi:
                plan, start = bodyz, bodyz.start
            else:
                at, n = loop.place[(slot, name)]
                base = body.plan.start[at] + ((body.b - 1) * per_batch[at] if body.plan is loop else 0)
                return at, base - (per_batch[at] - n)
            at, n = plan.place[(slot, name)]
            return at, start[at] + n

        def wait_items(eng, what, places):
            for at, n in dict(places).items():
                eng.wait_ge(what[at], n + 1)

        block = ctx.enter_context(nc.Block())

        @block.sync
        def _(sp):
            def load_x(b, c):
                sp.dma_start(x_stage[:, c % XS, :],
                             x_v[b, c // 2, :, (c % 2) * HALF:(c % 2 + 1) * HALF]
                             ).then_inc(x_loaded[c % XS], 16)

            sp.dma_start(raw_at[0], wqkv[0]).then_inc(raw_loaded[0], 16)
            for c in range(XS):
                load_x(0, c)
            sp.dma_start(neg_ident[:], consts[:, 0:P]).then_inc(const_loaded, 16)
            sp.dma_start(raw_mask, consts[0:2 * IT, P:P + 2 * HALF]).then_inc(const_loaded, 16)
            sp.dma_start(bias_sb[:], bias).then_inc(const_loaded, 16)
            sp.dma_start(scale_sb[:], scale).then_inc(const_loaded, 16)
            sp.dma_start(raw_at[VA], wqkv[VA]).then_inc(raw_loaded[VA], 16)
            for c in range(XS, 2 * KT):
                sp.wait_ge(x_split[c % 2], (c - XS) // 2 + 1)
                load_x(0, c)
            sp.dma_start(raw_at[1], wqkv[1]).then_inc(raw_loaded[1], 16)
            sp.dma_start(raw_wo, wout.rearrange("p a n -> p (a n)")).then_inc(raw_wo_loaded, 16)
            sp.dma_start(raw_at[2], wqkv[2]).then_inc(raw_loaded[2], 16)
            for n, c in enumerate((0, VA, 1)):
                sp.wait_ge(w_set, n + 1)
                sp.dma_start(w_split[c], w_ring[:, RING_OF[c]].rearrange("p h k n -> p (h k n)").bitcast(F32)
                             ).then_inc(spilled, 16)
                if c != 1:
                    late = {0: 3, VA: VB}[c]
                    sp.dma_start(raw_at[late], wqkv[late]).then_inc(raw_loaded[late], 16)
            for n, c in enumerate((2, 3, VB)):
                sp.wait_ge(spill_set, n + 1)
                sp.dma_start(w_split[c], spill.bitcast(F32)).then_inc(spilled_late, 16)
            sp.wait_ge(spilled, 48)
            sp.wait_ge(spilled_late, 48)

            def load_w(c):
                ring = RING_OF[c]
                sp.dma_start(w_ring[:, ring].rearrange("p h k n -> p (h k n)").bitcast(F32), w_split[c]
                             ).then_inc(w_loaded[ring], 16)

            def finish_half(b, half, after_x_load=False):
                done = b * 2 + half
                cols = slice(half * HALF, (half + 1) * HALF)
                if not after_x_load:
                    sp.wait_ge(out_stored, 16 * MT * done)
                for m in range(MT):
                    sp.dma_start(resid[:, m, :], x_v[b, m, :, cols]).then_inc(resid_loaded[m], 16)
                for m in range(MT):
                    sp.wait_ge(resid_added, 4 * done + m + 1)
                    sp.dma_start(out_v[b, m, :, cols], resid[:, m, :]).then_inc(out_stored, 16)

            def one(body):
                b = body.b
                wait_items(sp, aux_full, [earlier_at(body, 7, "V1")])
                load_w(2)
                body.full(sp, 0, "Q")
                load_w(VB)
                if not body.first:
                    finish_half(b - 1, 0, after_x_load=True)
                body.full(sp, 2, "Q")
                load_w(3)
                if not body.first:
                    finish_half(b - 1, 1)
                if not body.last:
                    body.full(sp, 2, "V1")
                    load_w(0)
                    body.full(sp, 4, "Q")
                    load_w(VA)
                    for c in range(XS - 1):
                        if c < 2:
                            sp.wait_ge(x_split[c], KT * (b + 1))
                        load_x(b + 1, c)
                    if not body.first:
                        sp.wait_ge(out_stored, 16 * MT * 2 * b)
                    load_x(b + 1, XS - 1)
                    body.full(sp, 6, "Q")
                    load_w(1)
                    for c in range(XS, 2 * KT):
                        sp.wait_ge(x_split[c % 2], KT * (b + 1) + (c - XS) // 2 + 1)
                        load_x(b + 1, c)

            run_bodies(sp, one)
            finish_half(B - 1, 0)
            finish_half(B - 1, 1)
            sp.wait_ge(out_stored, 16 * MT * 2 * B)

        @block.tensor
        def _(pe):
            def claim(body, slot, name, after=()):
                at, n = body.at(slot, name)
                if not (body.plan is pro and n == 0):
                    pe.wait_ge(aux_free[at], n)
                wait_items(pe, aux_free, [(a, i) for a, i in (body.at(*key) for key in after) if a != at])
                return at

            def wait_w(body, chunk, next_batch):
                ring = RING_OF[chunk]
                if body.plan is pro:
                    pe.wait_ge(w_set, {0: 1, VA: 2}[chunk])
                elif chunk in (0, 1, VA):
                    if body.first and not next_batch:
                        pe.wait_ge(w_set, 3)
                    else:
                        pe.wait_ge(w_loaded[ring], 16 * (2 * (body.b + (1 if next_batch else 0))))
                else:
                    pe.wait_ge(w_loaded[ring], 16 * (2 * body.b + 1))

            def project(out_ap, w, cols, xcols):
                n = 0
                for k in range(KT):
                    for wp, xp in ((0, x_hi), (1, x_hi), (0, x_lo)):
                        last = pe.matmul(out_ap, w[:, wp, k, cols], xp[:, k, xcols],
                                         start=(n == 0), stop=(n == 3 * KT - 1))
                        n += 1
                return last

            def item(body, slot, name):
                nslot = (slot + 1) % SLOTS
                npair, nhalf = divmod(nslot, 2)
                nb = slot == 7
                if name == "Q":
                    at = claim(body, slot, name)
                    if slot == 7:
                        for by in x_split:
                            pe.wait_ge(by, KT * (body.b + 2))
                    wait_w(body, npair, nb)
                    project(aux[at][:, 0:HALF], w_ring[:, RING_OF[npair]], slice(0, P),
                            slice(nhalf * HALF, (nhalf + 1) * HALF)).then_inc(aux_full[at], 1)
                elif name == "K":
                    kpair = (slot // 2 + 1) % PAIRS
                    at = claim(body, slot, name)
                    wait_w(body, kpair, nb)
                    for h in range(2):
                        last = project(aux[at][:, h * HALF:(h + 1) * HALF],
                                       w_ring[:, RING_OF[kpair]], slice(P, 2 * P),
                                       slice(h * HALF, (h + 1) * HALF))
                    last.then_inc(aux_full[at], 1)
                elif name in ("V0", "V1"):
                    chunk = VA if nb else VB
                    at = claim(body, slot, name)
                    wait_w(body, chunk, nb)
                    w = w_ring[:, RING_OF[chunk]]
                    for i in range(JT // 2):
                        jt = int(name[1]) * (JT // 2) + i
                        n = 0
                        for k in range(KT):
                            for wp, xp in ((0, x_hi), (1, x_hi), (0, x_lo)):
                                last = pe.matmul(aux[at][:, i * WCOLS:(i + 1) * WCOLS],
                                                 xp[:, k, jt * P:(jt + 1) * P], w[:, wp, k, :],
                                                 start=(n == 0), stop=(n == 3 * KT - 1))
                                n += 1
                    last.then_inc(aux_full[at], 1)
                elif name[0] == "M":
                    e, it = divmod(int(name[1]), IT)
                    after = []
                    if name == "M0":
                        after = [(slot, "Q")]
                        if nslot == 0:
                            after = [(slot, "Q"), (slot, "K")]
                        elif nhalf == 0:
                            after = [(slot - 1, "K"), (slot, "Q")]
                    at = claim(body, slot, name, after)
                    for h in range(2):
                        last = pe.matmul(aux[at][:, h * HALF:(h + 1) * HALF],
                                         q_hl[:, nhalf, e, it * P:(it + 1) * P],
                                         k_hh[:, npair % 2, e, h * HALF:(h + 1) * HALF],
                                         start=True, stop=True)
                    last.then_inc(aux_full[at], 1)
                elif name == "T":
                    at = claim(body, slot, name, [(slot, "M6"), (slot, "M7")])
                    pe.matmul(aux[at][0:2 * IT, 0:P], maxima[:], neg_ident[:],
                              start=True, stop=True).then_inc(aux_full[at], 1)
                elif name == "L":
                    done = body.b * SLOTS + slot
                    at = claim(body, slot, name)
                    pe.wait_ge(prob_added, 14 * done)
                    for e in range(2):
                        last = pe.matmul(aux[at][e * D:(e + 1) * D, 0:HALF], ones_d[:],
                                         prob_sum[:, e, :], start=True, stop=True)
                    last.then_inc(aux_full[at], 1)
                elif name in ("O0", "O1"):
                    done = body.b * SLOTS + slot
                    pair = (slot - 1) % SLOTS // 2
                    at = claim(body, slot, name)
                    if name == "O0":
                        pe.wait_ge(olo_ready, done)
                        if body.first and slot == 1:
                            pe.wait_ge(wo_set, 1)
                    for i in range(2):
                        m = 2 * int(name[1]) + i
                        for n, (w, o) in enumerate(((wo_hi, o_hi), (wo_lo, o_hi), (wo_hi, o_lo))):
                            last = pe.matmul(aux[at][:, i * HALF:(i + 1) * HALF],
                                             w[:, pair, m * P:(m + 1) * P], o[:],
                                             start=(n == 0), stop=(n == 2))
                    last.then_inc(aux_full[at], 1)
                else:
                    half = int(name[1]) if name != "R" else slot
                    batch = body.b if name in ("R0", "R1") else body.b - 1
                    at = claim(body, slot, name)
                    pe.wait_ge(sq_added, 3 * (2 * batch + half + 1))
                    pe.matmul(aux[at][:, 0:HALF], ones_c[:], sq_a[:], start=True, stop=True
                              ).then_inc(aux_full[at], 1)

            def scores(body, slot, j):
                pair, half = divmod(slot, 2)
                for e in range(2):
                    n = body.b * 128 + slot * 16 + 2 * j + e
                    if not (body.first and slot == 0 and j == 0):
                        pe.wait_ge(prob_ready, n - 1)
                    keys = slice(j * P, (j + 1) * P)
                    pe.matmul(score[e][:], k_hh[:, pair % 2, e, keys], q_hl[:, half, e, :],
                              start=True, stop=False)
                    pe.matmul(score[e][:], k_l1[0:D + 2 * IT, pair % 2, e, keys],
                              q_hm[0:D + 2 * IT, half, e, :], start=False, stop=True
                              ).then_inc(score_ready, 1)

            def values(body, slot, j, back):
                pair, half = divmod(slot, 2)
                b = body.b - 1 if back else body.b
                for e in range(2):
                    n = b * 128 + slot * 16 + 2 * j + e
                    pe.wait_ge(prob_ready, n + 1)
                    if j == 0 and e == 0 and not (body.first and slot < 2):
                        pe.wait_ge(onorm_ready, b * SLOTS + slot - 1)
                    pe.matmul(pv[half][e * D:(e + 1) * D, :],
                              v_sb[:, pair // 2, j, (pair % 2) * P + e * D:(pair % 2) * P + (e + 1) * D],
                              probs[:, j % 4, e, :], start=(j == 0), stop=(j == STEPS - 1)
                              ).then_inc(pv_done, 1)

            def one(body):
                for slot in range(SLOTS):
                    if slot == 0:
                        wait_items(pe, aux_free, [earlier_at(body, 7, n) for n in ("V0", "V1", "T")])
                    elif slot == 4:
                        wait_items(pe, aux_free, [body.at(1, "V0"), body.at(2, "V1"), body.at(3, "T")])
                    else:
                        body.consumed(pe, slot - 1, "T")
                    pe.wait_ge(q_repeated, body.b * SLOTS + slot + 1)
                    for t in range(HALF_STEPS):
                        j = t // 2
                        if t % 2 == 0:
                            scores(body, slot, j)
                        elif j > 0:
                            values(body, slot, j - 1, False)
                        elif slot > 0:
                            values(body, slot - 1, STEPS - 1, False)
                        elif not body.first:
                            values(body, SLOTS - 1, STEPS - 1, True)
                        for name in items_at(slot, t, body.first, body.last):
                            item(body, slot, name)

            pe.wait_ge(const_loaded, 64)
            pe.wait_ge(const_set, 3)
            start = Body(pro, -1, True, True)
            for name in PRO_ITEMS:
                item(start, 7, name)
            run_bodies(pe, one)
            end = Body(epi, B, False, True)
            values(end, SLOTS - 1, STEPS - 1, True)
            for name in ("L", "O0", "O1"):
                item(end, 0, name)
            last = Body(epi, B - 1, False, True)
            item(last, 0, "R0")
            item(last, 0, "R1")

        @block.scalar
        def _(act):
            def exponentials(body, slot, j):
                for e in range(2):
                    n = body.b * 128 + slot * 16 + 2 * j + e
                    act.wait_ge(score_ready, n + 1)
                    if not (body.first and slot == 0 and j < 4):
                        act.wait_ge(pv_done, n - 7)
                        base = (body.b * SLOTS + slot) * 14
                        added = base + (2 * max(j - 5, 0) + e + 1 if j >= 4 else 2 * (j + 3) + e + 1 - 14)
                        act.wait_ge(prob_added, added)
                    act.activation(probs[:, j % 4, e, :], score[e][:], ACT.Exp, scale=SOFT
                                   ).then_inc(prob_ready, 1)

            def repeat_queries(body, slot):
                nhalf = (slot + 1) % 2
                act.wait_ge(q_hi_ready, 2 * (SLOTS * body.b + slot + 2))
                act.activation(q_hm[0:D, nhalf, :, :], q_hl[0:D, nhalf, :, :].bitcast(F32),
                               ACT.Copy).then_inc(q_repeated, 1)

            def item(body, slot, name):
                nslot = (slot + 1) % SLOTS
                npair, nhalf = divmod(nslot, 2)
                if name == "Q":
                    at = body.full(act, slot, name)
                    for e in range(2):
                        act.activation(q_hl[0:D, nhalf, e, :], aux[at][e * D:(e + 1) * D, 0:HALF],
                                       ACT.Copy).then_inc(q_hi_ready, 1)
                    if body.plan is pro:
                        repeat_queries(body, slot)
                elif name == "K":
                    kpair = (slot // 2 + 1) % PAIRS
                    at = body.full(act, slot, name)
                    for e in range(2):
                        rows = slice(e * D, (e + 1) * D)
                        act.activation(k_hh[rows, kpair % 2, e, :], aux[at][rows, :], ACT.Copy
                                       ).then_inc(k_hi_ready, 1)
                elif name in ("V0", "V1"):
                    at = body.full(act, slot, name)
                    j0 = int(name[1]) * (JT // 2)
                    act.activation(v_sb[:, 0 if slot == 7 else 1, j0:j0 + JT // 2, :],
                                   aux[at][:].rearrange("p (j n) -> p j n", n=WCOLS), ACT.Copy
                                   ).then_inc(aux_free[at], 1)
                elif name in ("O0", "O1") and slot in (1, 2):
                    at = body.full(act, slot, name)
                    half = slot - 1
                    if name == "O0" and not body.first:
                        act.wait_ge(resid_added, 4 * (2 * (body.b - 1) + half + 1))
                    if name == "O0" and body.first and half == 0:
                        act.wait_ge(spilled_late, 48)
                    for i in range(2):
                        m = 2 * int(name[1]) + i
                        ins = act.activation(y_sb[:, half, m, :], aux[at][:, i * HALF:(i + 1) * HALF],
                                             ACT.Identity, bias=bias_sb[:, m:m + 1])
                    ins.then_inc(aux_free[at], 1)

            def split_output_high(done):
                act.wait_ge(onorm_ready, done)
                act.activation(o_hi[:], o_norm[:], ACT.Copy).then_inc(ohi_ready, 1)

            def square(body, half, m):
                done = 2 * (body.b - 1) + half
                if m == 0 and half == 0:
                    wait_items(act, aux_free, [earlier_at(body, 7, n) for n in ("O0", "O1")])
                elif m == 0:
                    if body.plan is epi:
                        Body(epi, B - 1, False, True).full(act, 0, "R0")
                    else:
                        body.full(act, 0, "R")
                    wait_items(act, aux_free, [body.at(0, n) for n in ("O0", "O1")])
                elif m >= 2:
                    act.wait_ge(sq_added, 3 * done + m - 1)
                act.activation((sq_a if m == 0 else sq_b)[:], y_sb[:, half, m, :], ACT.Square
                               ).then_inc(sq_made, 1)

            def root(done):
                act.wait_ge(inv_ms_ready, done + 1)
                act.activation(rms_a[:], rms_b[:], ACT.Sqrt).then_inc(rinv_ready, 1)
                act.activation(table_back[:], ones_d[:, 0:1], ACT.Exp)

            def split_x(c, n):
                act.wait_ge(x_loaded[c % XS], 16 * (n * 2 * KT // XS + c // XS + 1))
                act.activation(x_hi[:, c // 2, (c % 2) * HALF:(c % 2 + 1) * HALF],
                               x_stage[:, c % XS, :], ACT.Copy).then_inc(xhi_ready, 1)

            def one(body):
                for slot in range(SLOTS):
                    for t in range(HALF_STEPS):
                        if t % 2 == 0:
                            exponentials(body, slot, t // 2)
                        if (slot, t) in SCALE_AT and not body.first:
                            root(2 * (body.b - 1) + SCALE_AT.index((slot, t)))
                        for name in items_at(slot, t, body.first, body.last):
                            item(body, slot, name)
                        if t == REPEAT_AT and not (body.last and slot == SLOTS - 1):
                            repeat_queries(body, slot)
                        if t == NORMALISE_AT + 1 and not (body.first and slot == 0):
                            split_output_high(body.b * SLOTS + slot)
                        if t in SQUARE_AT and slot in (0, 1) and not body.first:
                            square(body, slot, SQUARE_AT.index(t))
                        if slot == 6 and not body.last and t in SPLIT_AT:
                            if t == SPLIT_AT[0]:
                                body.full(act, 6, "Q")
                            split_x(SPLIT_AT.index(t), body.b + 1)

            for c in range(2 * KT):
                split_x(c, 0)
            start = Body(pro, -1, True, True)
            act.wait_ge(const_loaded, 64)
            for name in PRO_ITEMS:
                item(start, 7, name)
            act.wait_ge(w_set, 3)
            act.wait_ge(wo_set, 1)
            act.wait_ge(spill_set, 1)
            run_bodies(act, one)
            end = Body(epi, B, False, True)
            split_output_high(B * SLOTS)
            for half in range(2):
                for m in range(MT):
                    square(end, half, m)
                root(2 * (B - 1) + half)

        @block.vector
        def _(dve):
            def item(body, slot, name):
                nslot = (slot + 1) % SLOTS
                npair, nhalf = divmod(nslot, 2)
                if name == "Q":
                    at = body.full(dve, slot, name)
                    before = SLOTS * body.b + slot + 1
                    for e in range(2):
                        dve.wait_ge(q_hi_ready, 2 * before + e + 1)
                        ins = dve.tensor_tensor(q_hl[D:2 * D, nhalf, e, :],
                                                aux[at][e * D:(e + 1) * D, 0:HALF],
                                                q_hl[0:D, nhalf, e, :].bitcast(F32), ALU.subtract)
                    ins.then_inc(aux_free[at], 1)
                elif name == "K":
                    at = body.full(dve, slot, name)
                    before = PAIRS * body.b + (slot + 1) // 2 + (slot != 7)
                    kp = (slot // 2 + 1) % PAIRS % 2
                    rows = [slice(e * D, (e + 1) * D) for e in range(2)]

                    def repeat_high(e):
                        dve.tensor_copy(k_hh[rows[1 - e], kp, e, :], k_hh[rows[e], kp, e, :].bitcast(F32))

                    for e in range(2):
                        dve.wait_ge(k_hi_ready, 2 * before + e + 1)
                        if slot == 7:
                            repeat_high(e)
                        ins = dve.tensor_tensor(k_l1[0:D, kp, e, :], aux[at][rows[e], :],
                                                k_hh[rows[e], kp, e, :].bitcast(F32), ALU.subtract)
                    ins.then_inc(aux_free[at], 1)
                    if slot != 7:
                        repeat_high(0)
                        repeat_high(1)
                elif name[0] == "M":
                    at = body.full(dve, slot, name)
                    n = int(name[1])
                    dve.tensor_reduce(maxima[:, n:n + 1], aux[at][:], AX_X, ALU.max
                                      ).then_inc(aux_free[at], 1)
                elif name == "T":
                    at = body.full(dve, slot, name)
                    dve.tensor_tensor(
                        q_hm[D:D + 2 * IT, nhalf].rearrange("t e (i n) -> t (e i) n", i=IT),
                        aux[at][0:2 * IT, 0:P].unsqueeze(1).to_broadcast([2 * IT, 2 * IT, P]),
                        tile_mask[:].rearrange("t (i n) -> t i n", i=2 * IT), ALU.mult
                    ).then_inc(aux_free[at], 1)
                elif name == "L":
                    at = body.full(dve, slot, name)
                    dve.reciprocal(inv_sum[:], aux[at][:, 0:HALF]).then_inc(aux_free[at], 1)
                elif name in ("O0", "O1") and slot not in (1, 2):
                    half, m = (slot - 1) % 2, 2 * int(name[1])
                    at = body.full(dve, slot, name)
                    if slot in (3, 4):
                        body.consumed(dve, slot - 2, name)
                    elif slot == 0:
                        wait_items(dve, aux_free, [earlier_at(body, 6, name)])
                    else:
                        body.consumed(dve, slot - 2, name)
                    y = y_sb[:, half, m:m + 2, :].rearrange("p m n -> p (m n)")
                    dve.tensor_tensor(y, y, aux[at][:], ALU.add).then_inc(aux_free[at], 1)
                elif name[0] == "R":
                    half = int(name[1]) if name != "R" else slot
                    batch = body.b if name in ("R0", "R1") else body.b - 1
                    done = 2 * batch + half
                    at = body.full(dve, slot, name)
                    if name == "R1":
                        dve.wait_ge(y_scaled, 4 * done)
                    dve.tensor_scalar(rms_a[:], aux[at][:, 0:HALF], SOFT, None, ALU.add
                                      ).then_inc(aux_free[at], 1)

            def invert(body, slot, name):
                body.consumed(dve, slot, name)
                dve.reciprocal(rms_b[:], rms_a[:]).then_inc(inv_ms_ready, 1)

            def normalise(body, slot):
                done = body.b * SLOTS + slot
                body.consumed(dve, slot, "L")
                dve.wait_ge(pv_done, 16 * done)
                dve.tensor_tensor(o_norm[:], inv_sum[:], pv[(slot - 1) % 2][:], ALU.mult
                                  ).then_inc(onorm_ready, 1)

            def add_square(done, m):
                dve.wait_ge(sq_made, 4 * done + m + 1)
                if m > 1:
                    dve.wait_ge(sq_added, 3 * done + m - 1)
                dve.tensor_tensor(sq_a[:], sq_a[:], sq_b[:], ALU.add).then_inc(sq_added, 1)

            def scale_y(done, half):
                dve.wait_ge(rinv_ready, done + 1)
                for m in range(MT):
                    dve.scalar_tensor_tensor(out=y_sb[:, half, m, :], in0=y_sb[:, half, m, :],
                                             scalar=scale_sb[:, m:m + 1], in1=rms_a[:],
                                             op0=ALU.mult, op1=ALU.mult).then_inc(y_scaled, 1)

            def split_w(n, c):
                dve.wait_ge(raw_loaded[c], 16)
                ring = w_ring[:, RING_OF[c]].rearrange("p h k n -> p h (k n)")
                dve.tensor_copy(ring[:, 0], raw_at[c]).then_inc(w_hi_set, 1)
                dve.wait_ge(w_hi_set, n + 1)
                dve.tensor_tensor(ring[:, 1], raw_at[c], ring[:, 0].bitcast(F32), ALU.subtract
                                  ).then_inc(w_set, 1)

            def one(body):
                for slot in range(SLOTS):
                    for t in range(HALF_STEPS):
                        if (slot, t) in SCALE_AT and not body.first:
                            half = SCALE_AT.index((slot, t))
                            scale_y(2 * (body.b - 1) + half, half)
                        for name in items_at(slot, t, body.first, body.last):
                            item(body, slot, name)
                        if (slot, t) in INVERT_AT and not body.first:
                            invert(body, INVERT_AT.index((slot, t)), "R")
                        if t == NORMALISE_AT and not (body.first and slot == 0):
                            normalise(body, slot)
                        if t == NORMALISE_AT + 2 and slot not in LOW_BY_GPSIMD:
                            split_output_low(dve, body.b * SLOTS + slot)
                        if t - 1 in SQUARE_AT[1:] and slot in (0, 1) and not body.first:
                            add_square(2 * (body.b - 1) + slot, SQUARE_AT.index(t - 1))
                        if slot == 6 and not body.last and t in SPLIT_AT[0::2]:
                            split_x(dve, SPLIT_AT.index(t), body.b + 1)

            dve.memset(ones_d[:], 1.0).then_inc(const_set, 1)
            dve.memset(ones_c[:], 1.0 / C).then_inc(const_set, 1)
            dve.memset(k_l1[D:D + 2 * IT].rearrange("p a e n -> p (a e n)").bitcast(F32), 1.0
                       ).then_inc(const_set, 1)
            split_w(0, 0)
            for c in range(0, 2 * KT, 2):
                split_x(dve, c, 0)
                if c == 2:
                    split_w(1, VA)
            split_w(2, 1)
            dve.wait_ge(const_loaded, 64)
            dve.tensor_copy(tile_mask[:], raw_mask).then_inc(mask_set, 1)
            dve.wait_ge(mask_set, 1)
            start = Body(pro, -1, True, True)
            for name in PRO_ITEMS:
                item(start, 7, name)
            run_bodies(dve, one)
            end = Body(epi, B, False, True)
            item(end, 0, "L")
            normalise(end, 0)
            for name in ("O0", "O1"):
                item(end, 0, name)
            last = Body(epi, B - 1, False, True)
            for half in range(2):
                for m in range(1, MT):
                    add_square(2 * (B - 1) + half, m)
                item(last, 0, f"R{half}")
                invert(last, 0, f"R{half}")
                scale_y(2 * (B - 1) + half, half)

        @block.gpsimd
        def _(pool):
            def add_probs(body, slot, j):
                base = (body.b * SLOTS + slot) * 14
                for e in range(2):
                    n = body.b * 128 + slot * 16 + 2 * j + e
                    pool.wait_ge(prob_ready, n + 1)
                    if j == 1:
                        if e == 0 and not (body.first and slot == 0):
                            body.full(pool, slot, "L")
                        pool.tensor_tensor(prob_sum[:, e, :], probs[:, 0, e, :], probs[:, 1, e, :],
                                           ALU.add).then_inc(prob_added, 1)
                    else:
                        pool.wait_ge(prob_added, base + 2 * (j - 2) + e + 1)
                        pool.tensor_tensor(prob_sum[:, e, :], prob_sum[:, e, :], probs[:, j % 4, e, :],
                                           ALU.add).then_inc(prob_added, 1)

            def add_resid(done, half, m):
                pool.wait_ge(y_scaled, 4 * done + m + 1)
                pool.wait_ge(resid_loaded[m], 16 * (done + 1))
                pool.tensor_tensor(resid[:, m, :], resid[:, m, :], y_sb[:, half, m, :],
                                   ALU.add).then_inc(resid_added, 1)

            def one(body):
                for slot in range(SLOTS):
                    for j in range(STEPS):
                        if j == OUTPUT_LOW_AT and slot in LOW_BY_GPSIMD and not (body.first and slot == 0):
                            split_output_low(pool, body.b * SLOTS + slot)
                        if j:
                            add_probs(body, slot, j)
                        if slot == 6 and not body.last:
                            for c in (1, 3, 5, 7):
                                if SPLIT_AT[c] // 2 == j:
                                    split_x(pool, c, body.b + 1)
                        if slot in (1, 2) and not body.first:
                            for m in range(MT):
                                if j == RESIDUAL_AT[slot - 1][m]:
                                    add_resid(2 * (body.b - 1) + slot - 1, slot - 1, m)

            for c in range(1, 2 * KT, 2):
                split_x(pool, c, 0)
            pool.wait_ge(raw_wo_loaded, 16)
            pool.tensor_copy(wo_hi[:].rearrange("p a n -> p (a n)"), raw_wo).then_inc(spill_hi_set, 1)
            pool.wait_ge(spill_hi_set, 1)
            pool.tensor_tensor(wo_lo[:].rearrange("p a n -> p (a n)"), raw_wo,
                               wo_hi[:].rearrange("p a n -> p (a n)").bitcast(F32), ALU.subtract
                               ).then_inc(wo_set, 1)
            for n, c in enumerate((2, 3, VB)):
                pool.wait_ge(raw_loaded[c], 16)
                if n:
                    pool.wait_ge(spilled_late, 16 * n)
                pool.tensor_copy(spill[:, 0:W1], raw_at[c]).then_inc(spill_hi_set, 1)
                pool.wait_ge(spill_hi_set, n + 2)
                pool.tensor_tensor(spill[:, W1:2 * W1], raw_at[c], spill[:, 0:W1].bitcast(F32),
                                   ALU.subtract).then_inc(spill_set, 1)
            run_bodies(pool, one)
            split_output_low(pool, B * SLOTS)
            for half in range(2):
                for m in range(MT):
                    add_resid(2 * (B - 1) + half, half, m)


def kernel(x, L0_conv_w_qkv, L0_conv_w_out, L0_conv_b_out, L0_conv_rms_scale):
    import concourse.bacc as bacc
    from concourse.bass_utils import run_bass_kernel_spmd

    x = np.ascontiguousarray(x)
    b, c, h, w = x.shape
    w_qkv, w_out = np.asarray(L0_conv_w_qkv), np.asarray(L0_conv_w_out)
    hid = w_out.shape[1]
    pairs = hid // P

    def chunk(rows):
        a = w_qkv[rows].reshape(len(rows), c // P, P)
        return a.transpose(2, 1, 0).reshape(P, -1)

    chunks = [chunk(np.r_[p * P:(p + 1) * P, hid + p * P:hid + (p + 1) * P]) for p in range(pairs)]
    chunks += [chunk(np.r_[2 * hid + s * 2 * P:2 * hid + (s + 1) * 2 * P]) for s in range(2)]
    consts = np.zeros((P, P + h * w), np.float32)
    consts[:, 0:P] = -np.eye(P, dtype=np.float32)
    for t in range(h * w // P):
        consts[t, P + t * P:P + (t + 1) * P] = 1.0
    arrays = {
        "x": x.reshape(b, c, h * w),
        "wqkv": np.ascontiguousarray(np.stack(chunks)),
        "wout": np.ascontiguousarray(w_out.T.reshape(pairs, P, c).transpose(1, 0, 2)),
        "bias": np.ascontiguousarray(np.asarray(L0_conv_b_out).reshape(c // P, P).T),
        "scale": np.ascontiguousarray(np.asarray(L0_conv_rms_scale).reshape(c // P, P).T),
        "consts": consts,
    }
    nc = bacc.Bacc("TRN2", target_bir_lowering=False, num_devices=1)
    args = [nc.dram_tensor(n, a.shape, mybir.dt.from_np(a.dtype), kind="ExternalInput").ap()
            for n, a in arrays.items()]
    out = nc.dram_tensor("out", (b, c, h * w), F32, kind="ExternalOutput").ap()
    attention_kernel(nc, *args, out)
    r = run_bass_kernel_spmd(nc, [arrays], core_ids=[0])
    return r.results[0]["out"].reshape(b, c, h, w)
```
